# Optimizing a Trainium2 kernel written in Bass

```python
import numpy as np
import jax
import jax.numpy as jnp

def _softmax(x, axis=-1):
    return jax.nn.softmax(x, axis=axis)

def _gelu(x):
    return jax.nn.gelu(x, approximate=True)

def _silu(x):
    return jax.nn.silu(x)

def _sigmoid(x):
    return jax.nn.sigmoid(x)

def _layernorm(x, axis=-1, eps=1e-05):
    m = jnp.mean(x, axis=axis, keepdims=True)
    v = jnp.var(x, axis=axis, keepdims=True)
    return (x - m) / jnp.sqrt(v + eps)

def _scatter_add(tgt, idx, src, axis=0):
    return tgt.at[idx].add(src)

def _segment_sum(src, seg, n):
    return jax.ops.segment_sum(src, seg, n)
kernel_name = 'mk_flamingo_gated_d1_seqx_r8_b9fb14'

def setup_inputs(seed: int=0):
    np.random.seed(seed)
    _w = jnp.asarray

    def _rec_inputs():
        import jax
        import jax.numpy as jnp
        _rk = jax.random.key(seed)
        x = -0.0002928 + 1 * jax.random.normal(jax.random.fold_in(_rk, 1), (128, 64, 128), jnp.float32)
        _lenS = 64 - jax.random.randint(jax.random.fold_in(_rk, 7), (128,), 0, max(1, 64 // 4) + 1, jnp.int32)
        _lenS2 = 64 - jax.random.randint(jax.random.fold_in(_rk, 8), (128,), 0, max(1, 64 // 4) + 1, jnp.int32)
        _ctx_1024P = jax.random.normal(jax.random.fold_in(_rk, 11), (128, 16, 128), jnp.float32)
        _ctx_1024c = jax.random.dirichlet(jax.random.fold_in(_rk, 511), 0.3 * jnp.ones((16,), jnp.float32), (128, 64))
        _ctx_1024t = jnp.einsum('bsk,bkd->bsd', _ctx_1024c, _ctx_1024P)
        _ctx_1024t = _ctx_1024t * jax.lax.rsqrt(jnp.mean(jnp.square(_ctx_1024t)) + 1e-12) * 0.953939
        ctx_1024 = -1.39393e-06 + 0.999914 * (_ctx_1024t + 0.3 * jax.random.normal(jax.random.fold_in(_rk, 611), (128, 64, 128), jnp.float32))
        fside_Bx1xSxS2_0 = -4.48278e-06 + 1.00019 * jax.random.normal(jax.random.fold_in(_rk, 12), (128, 1, 64, 64), jnp.float32)
        _g = jax.random.normal(jax.random.fold_in(_rk, 9001), (2, 1), jnp.float32)
        _g = jnp.sign(_g) * jnp.maximum(jnp.abs(_g), 1.0) + (_g == 0) * 1.0
        g_xattn = _g[0]
        g_ffn = _g[1]
        return (x, ctx_1024, fside_Bx1xSxS2_0, g_xattn, g_ffn)
    x, ctx_1024, fside_Bx1xSxS2_0, g_xattn, g_ffn = _rec_inputs()

    def _L0_xattn_setup():
        import jax, jax.numpy as jnp
        import numpy as np
        B, S, D_FF = (2, 256, 128)
        NUM_HEADS, D_KV = (16, 64)
        INNER = NUM_HEADS * D_KV
        key = jax.random.key(seed)
        ks = jax.random.split(key, 8)
        scale = 1.0 / np.sqrt(D_FF)
        return {'q': jax.random.normal(ks[0], (B, S, D_FF), jnp.float32), 'k': jax.random.normal(ks[1], (B, S, D_FF), jnp.float32), 'v': jax.random.normal(ks[2], (B, S, D_FF), jnp.float32), 'attn_mask': jax.random.normal(ks[3], (B, 1, S, S), jnp.float32), 'Wq': jax.random.normal(ks[4], (INNER, D_FF), jnp.float32) * scale, 'Wk': jax.random.normal(ks[5], (INNER, D_FF), jnp.float32) * scale, 'Wv': jax.random.normal(ks[6], (INNER, D_FF), jnp.float32) * scale, 'Wo': jax.random.normal(ks[7], (D_FF, INNER), jnp.float32) * scale, 'num_heads': NUM_HEADS}
    _L0_xattn_all = _L0_xattn_setup()
    _L0_xattn_in = {k: v for k, v in _L0_xattn_all.items() if k in ('Wq', 'Wk', 'Wv', 'Wo')}
    del _L0_xattn_all

    def _L0_ffn_setup():
        import jax, jax.numpy as jnp
        import numpy as np
        D_MODEL = 128
        NUM_EXPERTS = 8
        TOP_K = 2
        B, S = (4, 256)
        key = jax.random.key(seed)
        ks = jax.random.split(key, 7)
        scale_in = 1.0 / np.sqrt(D_MODEL)
        scale_hid = 1.0 / np.sqrt(2 * D_MODEL)
        return {'x': jax.random.normal(ks[0], (B, S, D_MODEL), dtype=jnp.float32), 'Wg': jax.random.normal(ks[1], (D_MODEL, NUM_EXPERTS), dtype=jnp.float32) * scale_in, 'bg': jnp.zeros((NUM_EXPERTS,), dtype=jnp.float32), 'W1': jax.random.normal(ks[2], (NUM_EXPERTS, D_MODEL, 2 * D_MODEL), dtype=jnp.float32) * scale_in, 'b1': jnp.zeros((NUM_EXPERTS, 2 * D_MODEL), dtype=jnp.float32), 'W2': jax.random.normal(ks[3], (NUM_EXPERTS, 2 * D_MODEL, D_MODEL), dtype=jnp.float32) * scale_hid, 'b2': jnp.zeros((NUM_EXPERTS, D_MODEL), dtype=jnp.float32)}
    _L0_ffn_all = _L0_ffn_setup()
    _L0_ffn_in = {k: v for k, v in _L0_ffn_all.items() if k in ('Wg', 'bg', 'W1', 'b1', 'W2', 'b2')}
    del _L0_ffn_all
    return {'x': x, 'ctx_1024': ctx_1024, 'fside_Bx1xSxS2_0': fside_Bx1xSxS2_0, 'g_xattn': g_xattn, 'g_ffn': g_ffn, 'L0_xattn_Wq': _L0_xattn_in['Wq'], 'L0_xattn_Wk': _L0_xattn_in['Wk'], 'L0_xattn_Wv': _L0_xattn_in['Wv'], 'L0_xattn_Wo': _L0_xattn_in['Wo'], 'L0_ffn_Wg': _L0_ffn_in['Wg'], 'L0_ffn_bg': _L0_ffn_in['bg'], 'L0_ffn_W1': _L0_ffn_in['W1'], 'L0_ffn_b1': _L0_ffn_in['b1'], 'L0_ffn_W2': _L0_ffn_in['W2'], 'L0_ffn_b2': _L0_ffn_in['b2']}

def reference(x, ctx_1024, fside_Bx1xSxS2_0, g_xattn, g_ffn, L0_xattn_Wq, L0_xattn_Wk, L0_xattn_Wv, L0_xattn_Wo, L0_ffn_Wg, L0_ffn_bg, L0_ffn_W1, L0_ffn_b1, L0_ffn_W2, L0_ffn_b2):
    import jax
    import jax.numpy as jnp

    def _L0_xattn_ref(q, k, v, attn_mask, Wq, Wk, Wv, Wo, num_heads):
        import jax, jax.numpy as jnp
        import numpy as np
        B, S, D_FF = (2, 256, 128)
        NUM_HEADS, D_KV = (16, 64)
        INNER = NUM_HEADS * D_KV
        b, s, _ = q.shape

        def proj_heads(x, W):
            y = jnp.einsum('bsd,ed->bse', x, W)
            return y.reshape(b, s, num_heads, -1).transpose(0, 2, 1, 3)
        qh = proj_heads(q, Wq)
        kh = proj_heads(k, Wk)
        vh = proj_heads(v, Wv)
        scores = jnp.einsum('bhqd,bhkd->bhqk', qh, kh) + attn_mask
        probs = jax.nn.softmax(scores, axis=-1)
        ctx = jnp.einsum('bhqk,bhkd->bhqd', probs, vh)
        ctx = ctx.transpose(0, 2, 1, 3).reshape(b, s, -1)
        return jnp.einsum('bse,de->bsd', ctx, Wo)

    def _L0_ffn_ref(x, Wg, bg, W1, b1, W2, b2):
        import jax, jax.numpy as jnp
        import numpy as np
        D_MODEL = 128
        NUM_EXPERTS = 8
        TOP_K = 2
        B, S = (4, 256)
        Bb, Ss, D = x.shape
        E = Wg.shape[1]
        xf = x.reshape(-1, D)
        logits = xf @ Wg + bg
        probs = jax.nn.softmax(logits, axis=-1)
        w, idx = jax.lax.top_k(probs, TOP_K)
        w = w / jnp.sum(w, axis=-1, keepdims=True)
        comb = jnp.sum(jax.nn.one_hot(idx, E, dtype=xf.dtype) * w[..., None], axis=1)
        h = jax.nn.relu(jnp.einsum('nd,edh->enh', xf, W1) + b1[:, None, :])
        y = jnp.einsum('enh,ehd->end', h, W2) + b2[:, None, :]
        out = jnp.einsum('end,ne->nd', y, comb)
        return out.reshape(Bb, Ss, D)
    x = x + jnp.tanh(g_xattn[0]) * _L0_xattn_ref(_layernorm(x, axis=-1), ctx_1024, ctx_1024, fside_Bx1xSxS2_0, L0_xattn_Wq, L0_xattn_Wk, L0_xattn_Wv, L0_xattn_Wo, 16)
    x = x + jnp.tanh(g_ffn[0]) * _L0_ffn_ref(_layernorm(x, axis=-1), L0_ffn_Wg, L0_ffn_bg, L0_ffn_W1, L0_ffn_b1, L0_ffn_W2, L0_ffn_b2)
    return x

_drawn_inputs = setup_inputs


def setup_inputs(seed=0):
    import zlib

    import numpy as np

    out = dict(_drawn_inputs(seed))
    spreads = {'L0_ffn_bg': (0.0, 0.1), 'L0_ffn_b1': (0.0, 0.42), 'L0_ffn_b2': (0.0, 0.294)}
    factors = {}
    for name, (base, spread) in spreads.items():
        noise = np.random.default_rng([zlib.crc32(name.encode()), seed]).standard_normal(out[name].shape)
        drawn = base * np.exp(spread * noise) if base else spread * noise
        out[name] = jnp.asarray(drawn.astype(out[name].dtype))
    for name, factor in factors.items():
        out[name] = (out[name] * factor).astype(out[name].dtype)
    return out
```

```python
from contextlib import ExitStack

import concourse.bass as bass
from concourse import mybir

F32 = mybir.dt.float32
F32R = mybir.dt.float32r
F16 = mybir.dt.float16
ALU = mybir.AluOpType
ACT = mybir.ActivationFunctionType
AX = mybir.AxisListType

B, S, D = 128, 64, 128
H, DV = 16, 64
E, HID = 8, 256
EPS = 1e-5
P = 128
N = 512
NBANK = 8
TILES = B // 2
GT = N // P
GB = N // S
GROUPS = B // GB
JG = H // 2
C = H * DV // P
HC = HID // P
WS = 32.0


ACT_ORDER = ("Q H", "hid relu", "hid H", "exp", "PT H", "PT out", "V H", "O H",
             "xT H", "ctxT H", "x2T H")
DVE_ORDER = ("y scaled", "sum", "inverse", "residual", "max", "shift", "Q L", "V place", "V L", "O L",
             "xT L", "ctxT L", "x2T L")
POOL_ORDER = ("normal", "y add", "hid L", "PT L")


class Line:

    def __init__(self, sem, done, order=()):
        self.sem, self.done, self.steps = sem, done, []
        self.rank = {kind: n for n, kind in enumerate(order)}
        self.slot, self.queued = 0, []

    def step(self, name, after, work):
        rank = self.rank.get(name[0], len(self.rank)) if self.slot else 0
        self.queued.append((self.slot, rank, name, after, work))

    def number(self):
        self.queued.sort(key=lambda q: q[:2])
        for _, _, name, after, work in self.queued:
            self.steps.append((after, work))
            assert name not in self.done, name
            self.done[name] = (self.sem, len(self.steps))

    def emit(self, eng):
        passed = {}
        for after, work in self.steps:
            for name in after:
                sem, count = self.done[name]
                if passed.get(sem.name, 0) < count:
                    passed[sem.name] = count
                    eng.wait_ge(sem, count)
            work(eng).then_inc(self.sem, 1)


class Loads:

    def __init__(self, done):
        self.done, self.steps, self.count = done, [], {}

    def dma(self, name, sem, after, out, in_):
        self.count[sem.name] = self.count.get(sem.name, 0) + 16
        self.done[name] = (sem, self.count[sem.name])
        self.steps.append((after, sem, out, in_))

    def emit(self, eng):
        passed = {}
        for after, sem, out, in_ in self.steps:
            for name in after:
                wait_sem, count = self.done[name]
                if passed.get(wait_sem.name, 0) < count:
                    passed[wait_sem.name] = count
                    eng.wait_ge(wait_sem, count)
            eng.dma_start(out, in_).then_inc(sem, 16)


def flamingo_block(nc, x, ctx, mask, g_xattn, g_ffn, Wq, Wk, Wv, Wo, Wg, bg, W1, b1, W2, b2, out):
    stack = ExitStack()
    with stack:
        def sb(name, shape, dt=F32):
            return stack.enter_context(nc.sbuf_tensor(name, shape, dt))

        def sem(name):
            return stack.enter_context(nc.semaphore(name))

        ident = sb("ident", [P, P])
        spread = sb("spread", [P, P], F32R)
        tri = sb("tri", [P, E, E])
        aH, aL = (sb(f"a{p}", [P, H, D], F16) for p in "HL")
        wvH, wvL = (sb(f"wv{p}", [P, H * DV], F16) for p in "HL")
        woH, woL = (sb(f"wo{p}", [P, C, D], F16) for p in "HL")
        w1H, w1L = (sb(f"w1{p}", [P, E, HID], F16) for p in "HL")
        w2H, w2L = (sb(f"w2{p}", [P, E, HC, D], F16) for p in "HL")
        wgH, wgL = (sb(f"wg{p}", [P, E], F16) for p in "HL")
        b1col = sb("b1col", [P, E, HC])
        b2rows = sb("b2rows", [2, E, D], F32R)
        kilo2 = sb("kilo2", [2, P], F32R)
        bgrow = sb("bgrow", [P, E])
        gates = sb("gates", [P, 2])
        tanh_gates = sb("tanh_gates", [P, 2])
        out_scale = sb("out_scale", [P, 2])

        NX = 4
        x_raw = sb("x_raw", [P, NX, GT, D])
        ctx_raw = sb("ctx_raw", [P, 2, GT, D])
        mask_raw = sb("mask_raw", [P, GB, S])
        mask_parts = sb("mask_parts", [P, 2, GB, S], F32R)
        stats = sb("stats", [P, 2, GT, 6])
        meanvar = sb("meanvar", [P, 2, GT, 2])
        rstd = sb("rstd", [P, 2, GT])
        minus_half = sb("minus_half", [P, GT])
        xhat = sb("xhat", [P, GT, D])
        x2hat = sb("x2hat", [P, GT, D])
        xtH, xtL = (sb(f"xt{p}", [P, 2, N], F16) for p in "HL")
        ctH, ctL = (sb(f"ct{p}", [P, 2, N], F16) for p in "HL")
        x2tH, x2tL = (sb(f"x2t{p}", [P, 2, N], F16) for p in "HL")
        qH, qL = (sb(f"q{p}", [P, 2, JG, GB, 2, S], F16) for p in "HL")
        NX2 = 3
        x2 = sb("x2", [P, NX2, GT, D])

        NPB = 3
        prob = sb("prob", [P, NPB, JG, S])
        row_max = sb("row_max", [P, NPB, JG])
        row_sum = sb("row_sum", [P, NPB, JG])
        row_inv = sb("row_inv", [P, NPB, JG])
        pt = sb("pt", [P, 2, N])
        ptH, ptL = (sb(f"pt{p}", [P, 2, N], F16) for p in "HL")
        vH, vL = (sb(f"v{p}", [P, C, 2, DV], F16) for p in "HL")
        vdH, vdL = (sb(f"vd{p}", [P, 2, 2, C, 2, DV], F16) for p in "HL")
        otH, otL = (sb(f"ot{p}", [P, 2, C, 2, S], F16) for p in "HL")

        logit_t = sb("logit_t", [E, N])
        logit = sb("logit", [P, 2, GT, E])
        logit_max = sb("logit_max", [P, 2, GT])
        expo = sb("expo", [P, 2, GT, E])
        above = sb("above", [P, GT, E, E])
        same = sb("same", [P, GT, E, E])
        rank = sb("rank", [P, GT, E])
        picked = sb("picked", [P, GT, E])
        picked_sum = sb("picked_sum", [P, GT])
        picked_inv = sb("picked_inv", [P, GT])
        comb = sb("comb", [P, 2, GT, E])
        NR = 3
        hid = sb("hid", [P, NR, N])
        hidH, hidL = (sb(f"hid{p}", [P, 2, HC, N], F16) for p in "HL")
        y_scaled = sb("y_scaled", [P, 2, GT, D])

        q_bytes = [q[:, :, :, :, :, :].rearrange("p a b c d e -> p (a b c d e)").bitcast(F32) for q in (qH, qL)]
        wq_raw = q_bytes[0][0:DV, 0:2048].rearrange("p (h d) -> p h d", h=H)
        wk_raw = q_bytes[0][0:DV, 2048:4096].rearrange("p (h d) -> p h d", h=H)
        wv_raw = q_bytes[0][:, 4096:5120].rearrange("p (c d) -> p c d", c=C)
        wo_raw = q_bytes[0][:, 5120:6144].rearrange("p (c d) -> p c d", c=C)
        b1_raw = q_bytes[0][0:E * HC, 6144:6144 + P]
        wg_raw = q_bytes[0][:, 6272:6272 + E]
        w1_raw = q_bytes[1][:, 0:2048].rearrange("p (e n) -> p e n", e=E)
        w2_raw = q_bytes[1][:, 2048:4096].rearrange("p (e c d) -> p e c d", e=E, c=HC)
        b2_raw = q_bytes[1][0:2, 4096:5120].rearrange("p (e d) -> p e d", e=E)
        b2_low = q_bytes[1][0:2, 5120:6144].rearrange("p (e d) -> p e d", e=E)

        bank = [stack.enter_context(nc.psum_tensor(f"bank{i}", [P, N], F32)) for i in range(NBANK)]

        done = {}
        pe = Line(sem("pe_steps"), done)
        act = Line(sem("act_steps"), done, ACT_ORDER)
        dve = Line(sem("dve_steps"), done, DVE_ORDER)
        pool = Line(sem("pool_steps"), done, POOL_ORDER)
        sp = Loads(done)
        s_load = {k: [sem(f"load_{k}{i}") for i in range(n)]
                  for k, n in (("x", NX), ("ctx", 2), ("mask", 1), ("w", 12), ("out", 2))}

        uses = []
        bank_of = {}

        def take(name, freed_by):
            n = len(uses)
            uses.append(freed_by)
            bank_of[name] = bank[n % NBANK]
            return [uses[n - NBANK]] if n >= NBANK else []

        def bk(name):
            return bank_of[name]

        def load_weights():
            for n, (name, dst, src) in enumerate([
                ("Wq", wq_raw, Wq.rearrange("(h e) d -> e h d", h=H)),
                ("Wk", wk_raw, Wk.rearrange("(h e) d -> e h d", h=H)),
                ("Wv", wv_raw, Wv.rearrange("(c p) d -> p c d", p=P)),
                ("Wo", wo_raw, Wo.rearrange("d (c p) -> d c p", p=P)),
                ("W1", w1_raw, W1.rearrange("e d n -> d e n")),
                ("W2", w2_raw, W2.rearrange("e (c p) d -> p e c d", p=P)),
                ("Wg", wg_raw, Wg),
                ("b1", b1_raw, b1.rearrange("e (c p) -> (e c) p", p=P)),
            ]):
                sp.dma(name, s_load["w"][n], [], dst, src)
            sp.dma("b2", s_load["w"][8], [], b2_raw, b2.unsqueeze(0).to_broadcast([2, E, D]))
            sp.dma("bg", s_load["w"][9], [], bgrow[:, :], bg.unsqueeze(0).to_broadcast([P, E]))
            sp.dma("g_xattn", s_load["w"][10], [], gates[:, 0:1], g_xattn.unsqueeze(0).to_broadcast([P, 1]))
            sp.dma("g_ffn", s_load["w"][11], [], gates[:, 1:2], g_ffn.unsqueeze(0).to_broadcast([P, 1]))

        def constants():
            pool.step("ident zero", [], lambda e: e.memset(ident[:, :], 0.0))
            pool.step("ident", ["ident zero"], lambda e: e.affine_select(
                out=ident[:, :], in_=ident[:, :], compare_op=ALU.not_equal, fill=1.0, base=0,
                pattern=[[-1, P]], channel_multiplier=1))
            pool.step("tri one", [], lambda e: e.memset(tri[:, :, :], 1.0))
            pool.step("tri", ["tri one"], lambda e: e.affine_select(
                out=tri[:, :, :], in_=tri[:, :, :], compare_op=ALU.is_gt, fill=0.0, base=0,
                pattern=[[1, E], [-1, E]], channel_multiplier=0))
            pool.step("minus_half", [], lambda e: e.memset(minus_half[:, :], -0.5))
            pool.step("V zero H", [], lambda e: e.memset(vdH[:, :, :, :, :, :], 0.0))
            pool.step("V zero L", [], lambda e: e.memset(vdL[:, :, :, :, :, :], 0.0))

            def spread_work(e):
                for half in (slice(0, S), slice(S, P)):
                    for col in (slice(0, S), slice(S, P)):
                        last = e.tensor_scalar(spread[half, col], ident[half, half], WS, None, ALU.mult)
                return last
            dve.step("spread", ["ident"], spread_work)
            dve.step("kilo2", ["ident"], lambda e: e.tensor_scalar(
                kilo2[:, :], ident[0:2, :], 0.0, WS * WS, ALU.mult, ALU.add))
            act.step("tanh gates", ["g_xattn", "g_ffn"], lambda e: e.activation(
                tanh_gates[:, :], gates[:, :], ACT.Tanh))
            dve.step("out_scale", ["tanh gates"], lambda e: e.tensor_scalar(
                out_scale[:, :], tanh_gates[:, :], 1.0 / (WS * WS), None, ALU.mult))

        def parts_of(name, src, after, dst_high, dst_low, scale=WS):
            act.step((name, "H"), after, lambda e: e.activation(dst_high, src(), ACT.Copy, scale=scale))
            dve.step((name, "L"), [(name, "H")], lambda e: e.scalar_tensor_tensor(
                dst_low, src(), scale, dst_high, ALU.mult, ALU.subtract))

        def prepare_weights():
            for n in range(H // 4):
                name = ("A", n)

                def work(e, n=n, name=name):
                    for i in range(4):
                        last = e.matmul(bk(name)[:, i * D:(i + 1) * D], wq_raw[:, 4 * n + i, :],
                                        wk_raw[:, 4 * n + i, :], start=True, stop=True)
                    return last
                pe.step(name, take(name, (name, "L")) + ["Wq", "Wk"], work)
                flat = [a[:, 4 * n:4 * n + 4, :].rearrange("p h d -> p (h d)") for a in (aH, aL)]
                parts_of(name, lambda name=name: bk(name)[:, :], [name], *flat)
            for what, raw, high, low in (("Wv", wv_raw, wvH[:, :], wvL[:, :]),
                                         ("Wo", wo_raw, woH[:, :, :].rearrange("p c d -> p (c d)"),
                                          woL[:, :, :].rearrange("p c d -> p (c d)"))):
                for n in range(C // 4):
                    name = (what + "T", n)

                    def work(e, n=n, name=name, raw=raw):
                        for i in range(4):
                            last = e.transpose(bk(name)[:, i * P:(i + 1) * P], raw[:, 4 * n + i, :], ident[:, :])
                        return last
                    pe.step(name, take(name, (name, "L")) + [what, "ident"], work)
                    parts_of(name, lambda name=name: bk(name)[:, :], [name],
                             high[:, n * N:(n + 1) * N], low[:, n * N:(n + 1) * N])
            pe.step("b1T", take("b1T", "b1col") + ["b1", "ident"], lambda e: e.transpose(
                bk("b1T")[:, 0:E * HC], b1_raw, ident[0:E * HC, 0:E * HC]))
            act.step("b1col", ["b1T"], lambda e: e.activation(
                b1col[:, :, :].rearrange("p e c -> p (e c)"), bk("b1T")[:, 0:E * HC], ACT.Copy, scale=WS))
            parts_of("Wg parts", lambda: wg_raw, ["Wg"], wgH[:, :], wgL[:, :])
            parts_of("W1 parts", lambda: w1_raw.rearrange("p e n -> p (e n)"), ["W1"],
                     w1H[:, :, :].rearrange("p e n -> p (e n)"), w1L[:, :, :].rearrange("p e n -> p (e n)"))
            parts_of("W2 parts", lambda: w2_raw.rearrange("p e c d -> p (e c d)"), ["W2"],
                     w2H[:, :, :, :].rearrange("p e c d -> p (e c d)"),
                     w2L[:, :, :, :].rearrange("p e c d -> p (e c d)"))
            dve.step("b2 high", ["b2"], lambda e: e.tensor_copy(b2rows[:, :, :], b2_raw))
            dve.step("b2 low", ["b2 high"], lambda e: e.tensor_tensor(
                b2_low, b2_raw, b2rows[:, :, :], ALU.subtract))
            dve.step("b2 row 1", ["b2 low", "ident"], lambda e: e.tensor_scalar(
                b2_low, b2_low, ident[0:2, 1:2], None, ALU.mult))
            dve.step("b2rows", ["b2 row 1"], lambda e: e.scalar_tensor_tensor(
                b2rows[:, :, :], b2rows[:, :, :], ident[0:2, 0:1], b2_low, ALU.mult, ALU.add))

        weights_read = ([((w, n), "L") for w, m in (("A", H // 4), ("WvT", C // 4), ("WoT", C // 4))
                         for n in range(m)] + ["b1col", ("Wg parts", "L"), ("W1 parts", "L"),
                                               ("W2 parts", "L"), "b2rows"])

        def load_x(g):
            after = [("residual", GT * (g - NX) + GT - 1)] if g >= NX else []
            sp.dma(("x", g), s_load["x"][g % NX], after, x_raw[:, g % NX, :, :],
                   x[GB * g:GB * (g + 1)].rearrange("(t b) q d -> (b q) t d", b=2))

        def load_ctx(g):
            after = [("ctxT", g - 2)] if g >= 2 else []
            sp.dma(("ctx", g), s_load["ctx"][g % 2], after, ctx_raw[:, g % 2, :, :],
                   ctx[GB * g:GB * (g + 1)].rearrange("(t b) q d -> (b q) t d", b=2))

        def load_mask(g):
            after = [("mask low", g - 1)] if g >= 1 else []
            for half in range(2):
                sp.dma(("mask", g, half), s_load["mask"][0], after, mask_raw[half * S:(half + 1) * S, :, :],
                       mask[GB * g:GB * (g + 1), 0].rearrange("b q k -> q b k"))

        def mask_split(g):
            parts = mask_parts[:, g % 2, :, :]
            dve.step(("mask high", g), [("mask", g, 0), ("mask", g, 1)]
                     + ([("scores", GB * (g - 1) - 1)] if g >= 2 else []),
                     lambda e: e.tensor_copy(parts, mask_raw[:, :, :]))
            dve.step(("mask low", g), [("mask high", g)], lambda e: e.tensor_tensor(
                parts[S:P], mask_raw[S:P, :, :], parts[S:P], ALU.subtract))

        def norm_steps(which, g, src, dst, after, dst_free):
            st, mv, rs = stats[:, which], meanvar[:, which], rstd[:, which]
            n = ("LN", which, g)

            def stats_work(e):
                for t in range(GT):
                    last = e.bn_stats(st[:, t, :], src[:, t, :])
                return last

            def aggr_work(e):
                for t in range(GT):
                    last = e.bn_aggr(mv[:, t, :], st[:, t, :])
                return last

            def rows_work(e):
                for t in range(GT):
                    last = e.tensor_scalar(dst[:, t, :], src[:, t, :], mv[:, t, 0:1], rs[:, t:t + 1],
                                           ALU.subtract, ALU.mult)
                return last
            prior = [("LN", which, g - 1, "rows")] if g else []
            return [
                lambda: dve.step(n + ("stats",), after + prior, stats_work),
                lambda: dve.step(n + ("aggr",), [n + ("stats",)], aggr_work),
                lambda: (
                    dve.step(n + ("var",), [n + ("aggr",)], lambda e: e.tensor_scalar(
                        rs, mv[:, :, 1], EPS, None, ALU.add)),
                    pool.step(n + ("rstd",), [n + ("var",), "minus_half"], lambda e: e.tensor_tensor(
                        rs, rs, minus_half[:, :], ALU.pow))),
                lambda: dve.step(n + ("rows",), [n + ("rstd",)] + dst_free, rows_work),
            ]

        def transpose_group(name, g, src, after, high, low, free):
            n = (name, g)

            def work(e):
                for t in range(GT):
                    last = e.transpose(bk(n)[:, t * P:(t + 1) * P], src[:, t, :], ident[:, :])
                return last
            pe.step(n, take(n, (name + " L", g)) + after + ["ident"], work)
            act.step((name + " H", g), [n] + free, lambda e: e.activation(high, bk(n)[:, :], ACT.Copy))
            dve.step((name + " L", g), [(name + " H", g)], lambda e: e.tensor_tensor(
                low, bk(n)[:, :], high, ALU.subtract))

        def three_passes(e, dst, lhs, rhs, start=True, stop=True):
            e.matmul(dst, lhs[0], rhs[0], start=start, stop=False, skip_group_check=True)
            e.matmul(dst, lhs[0], rhs[1], start=False, stop=False, skip_group_check=True)
            return e.matmul(dst, lhs[1], rhs[0], start=False, stop=stop, skip_group_check=True)

        def project_queries(g, h):
            n = ("Q", g, h)
            j, h2, g2 = h // 4, h % 4 // 2, h % 2
            after = [("xT L", g)] + ([(("A", h // 4), "L")])
            pe.step(n, take(n, ("Q L", g, h)) + after, lambda e: three_passes(
                e, bk(n)[:, :], (aH[:, h, :], aL[:, h, :]), (xtH[:, g % 2, :], xtL[:, g % 2, :])))
            dst = [q[:, g % 2, 2 * j + g2, :, h2, :] for q in (qH, qL)]
            src = lambda: bk(n)[:, :].rearrange("p (b q) -> p b q", b=GB)
            free = [("scores", GB * (g - 1) - 1)] if g >= 2 else weights_read
            act.step(("Q H", g, h), [n] + free, lambda e: e.activation(dst[0], src(), ACT.Copy))
            dve.step(("Q L", g, h), [("Q H", g, h)], lambda e: e.tensor_tensor(
                dst[1], src(), dst[0], ALU.subtract))

        def scores(b):
            n = ("scores", b)
            g, i = b // GB, b % GB

            def work(e):
                cols = slice(i * S, (i + 1) * S)
                e.matmul(bk(n)[:, :].rearrange("p (j k) -> p j k", j=JG), spread[:, :],
                         mask_parts[:, g % 2, i, :].unsqueeze(1).to_broadcast([P, JG, S]),
                         start=True, stop=False, skip_group_check=True)
                for jg in range(JG):
                    lhs = [q[:, g % 2, jg, i, :, :].rearrange("p a q -> p (a q)") for q in (qH, qL)]
                    last = three_passes(e, bk(n)[:, jg * S:(jg + 1) * S], lhs,
                                        (ctH[:, g % 2, cols], ctL[:, g % 2, cols]), start=False)
                return last
            pe.step(n, take(n, ("shift", b)) + [("Q L", g, H - 1), ("ctxT L", g), ("mask low", g), "spread"], work)

        def softmax_max(b):
            src = lambda: bk(("scores", b))[:, :].rearrange("p (j k) -> p j k", j=JG)
            dve.step(("max", b), [("scores", b)] + ([("shift", b - NPB)] if b >= NPB else []),
                     lambda e: e.tensor_reduce(row_max[:, b % NPB, :], src(), AX.X, ALU.max))

        def softmax_shift(b):
            src = lambda: bk(("scores", b))[:, :].rearrange("p (j k) -> p j k", j=JG)
            dve.step(("shift", b), [("max", b)] + ([("PT", b - NPB)] if b >= NPB else []),
                     lambda e: e.tensor_tensor(
                         prob[:, b % NPB, :, :], src(),
                         row_max[:, b % NPB, :].unsqueeze(2).to_broadcast([P, JG, S]), ALU.subtract))

        def softmax_exp(b):
            p = prob[:, b % NPB, :, :]
            act.step(("exp", b), [("shift", b)], lambda e: e.activation(p, p, ACT.Exp, scale=1.0 / WS))

        def softmax_sum(b):
            p = prob[:, b % NPB, :, :]
            dve.step(("sum", b), [("exp", b)] + ([("inverse", b - NPB)] if b >= NPB else []),
                     lambda e: e.tensor_reduce(row_sum[:, b % NPB, :], p, AX.X, ALU.add))

        def softmax_inverse(b):
            dve.step(("inverse", b), [("sum", b)] + ([("normal", b - NPB)] if b >= NPB else []),
                     lambda e: e.reciprocal(row_inv[:, b % NPB, :], row_sum[:, b % NPB, :]))

        def softmax_normal(b):
            p = prob[:, b % NPB, :, :]
            pool.step(("normal", b), [("inverse", b)], lambda e: e.tensor_tensor(
                p, p, row_inv[:, b % NPB, :].unsqueeze(2).to_broadcast([P, JG, S]), ALU.mult))

        def transpose_probs(b):
            n = ("PT", b)

            def work(e):
                p = prob[:, b % NPB, :, :].rearrange("p j k -> p (j k)")
                for j in range(4):
                    last = e.transpose(bk(n)[:, j * P:(j + 1) * P], p[:, j * P:(j + 1) * P], ident[:, :])
                return last
            pe.step(n, take(n, ("PT out", b)) + [("normal", b)], work)

        def probs_high(b):
            act.step(("PT H", b), [("PT", b)] + ([("PV", b - 2)] if b >= 2 else []),
                     lambda e: e.activation(ptH[:, b % 2, :], bk(("PT", b))[:, :], ACT.Copy))
            act.step(("PT out", b), [("PT", b)] + ([("PT L", b - 2)] if b >= 2 else []),
                     lambda e: e.activation(pt[:, b % 2, :], bk(("PT", b))[:, :], ACT.Copy))

        def probs_low(b):
            pool.step(("PT L", b), [("PT out", b)], lambda e: e.tensor_tensor(
                ptL[:, b % 2, :], pt[:, b % 2, :], ptH[:, b % 2, :], ALU.subtract))

        def project_values(t):
            g, i = t // GT, t % GT
            for half in range(2):
                n = ("V", t, half)
                cols = slice(half * N, (half + 1) * N)
                pe.step(n, take(n, ("V L", t, half)) + [("ctxT L", g), (("WvT", 1), "L")],
                        lambda e, n=n, cols=cols: three_passes(
                            e, bk(n)[:, :], [c[:, g % 2, i * P:(i + 1) * P] for c in (ctH, ctL)],
                            (wvH[:, cols], wvL[:, cols])))

        def values_parts(t):
            for half in range(2):
                n = ("V", t, half)
                dst = [v[:, 4 * half:4 * half + 4, :, :].rearrange("p c g d -> p (c g d)") for v in (vH, vL)]
                act.step(("V H", t, half), [n] + ([("V place", t - 1)] if t else []),
                         lambda e, n=n, dst=dst: e.activation(dst[0], bk(n)[:, :], ACT.Copy))
                dve.step(("V L", t, half), [("V H", t, half)], lambda e, n=n, dst=dst: e.tensor_tensor(
                    dst[1], bk(n)[:, :], dst[0], ALU.subtract))

        def values_place(t):
            def work(e):
                for src, dst in ((vH, vdH), (vL, vdL)):
                    for b2 in range(2):
                        for g2 in range(2):
                            last = e.tensor_copy(dst[g2 * S:(g2 + 1) * S, t % 2, b2, :, g2, :],
                                                 src[b2 * S:(b2 + 1) * S, :, g2, :])
                return last
            dve.step(("V place", t), [("V L", t, 1), "V zero H", "V zero L"]
                     + ([("PV", 2 * t - 3)] if t >= 2 else []), work)

        def probs_values(b):
            n = ("PV", b)
            t = b // 2

            def work(e):
                for c in range(C):
                    cols = slice(c * S, (c + 1) * S)
                    lhs = [v[:, t % 2, b % 2, c, :, :].rearrange("p g d -> p (g d)") for v in (vdH, vdL)]
                    last = three_passes(e, bk(n)[:, cols], lhs, (ptH[:, b % 2, cols], ptL[:, b % 2, cols]))
                return last
            pe.step(n, take(n, ("O L", b)) + [("PT L", b), ("V place", t)], work)

        def heads_parts(b):
            t = b // 2
            dst = [o[:, t % 2, :, b % 2, :] for o in (otH, otL)]
            src = lambda: bk(("PV", b))[:, :].rearrange("p (c q) -> p c q", c=C)
            act.step(("O H", b), [("PV", b)] + ([("Wo", t - 2)] if t >= 2 else []),
                     lambda e: e.activation(dst[0], src(), ACT.Copy))
            dve.step(("O L", b), [("O H", b)], lambda e: e.tensor_tensor(dst[1], src(), dst[0], ALU.subtract))

        def project_out(t):
            n = ("Wo", t)

            def work(e):
                for c in range(C):
                    lhs = [o[:, t % 2, c, :, :].rearrange("p b q -> p (b q)") for o in (otH, otL)]
                    last = three_passes(e, bk(n)[:, 0:D], lhs, (woH[:, c, :], woL[:, c, :]),
                                        start=(c == 0), stop=(c == C - 1))
                return last
            pe.step(n, take(n, ("residual", t)) + [("O L", 2 * t + 1), (("WoT", 1), "L")], work)

        def residual(t):
            g, i = t // GT, t % GT
            free = [("store", g - NX2)] if g >= NX2 else []
            dve.step(("residual", t), [("Wo", t), ("x", g), "out_scale"] + free,
                     lambda e: e.scalar_tensor_tensor(x2[:, g % NX2, i, :], bk(("Wo", t))[:, 0:D],
                                                      out_scale[:, 0:1], x_raw[:, g % NX, i, :],
                                                      ALU.mult, ALU.add))

        def gate_logits(g):
            n = ("logitT", g)
            pe.step(n, take(n, ("logitT out", g)) + [("x2T L", g), ("Wg parts", "L")],
                    lambda e: three_passes(e, bk(n)[0:E, :], (wgH[:, :], wgL[:, :]),
                                           (x2tH[:, g % 2, :], x2tL[:, g % 2, :])))
            act.step(("logitT out", g), [n] + ([("logit", g - 1)] if g else []),
                     lambda e: e.activation(logit_t[:, :], bk(n)[0:E, :], ACT.Copy, scale=1.0 / WS))

        def gate_rows(g):
            n = ("logit", g)

            def work(e):
                for t in range(GT):
                    last = e.transpose(bk(n)[:, t * E:(t + 1) * E], logit_t[:, t * P:(t + 1) * P], ident[0:E, 0:E])
                return last
            pe.step(n, take(n, ("logit in", g)) + [("logitT out", g)], work)
            l, m, x_ = logit[:, g % 2], logit_max[:, g % 2], expo[:, g % 2]
            dve.step(("logit in", g), [n, "bg"] + ([("rank eq", g - 2), ("gate shift", g - 2)] if g >= 2 else []),
                     lambda e: e.tensor_tensor(
                         l, bk(n)[:, 0:GT * E].rearrange("p (t e) -> p t e", t=GT),
                         bgrow[:, :].unsqueeze(1).to_broadcast([P, GT, E]), ALU.add))
            prior = [("picked", g - 1)] if g else []
            lj = l.unsqueeze(2).to_broadcast([P, GT, E, E])
            li = l.unsqueeze(3).to_broadcast([P, GT, E, E])
            dve.step(("rank gt", g), [("logit in", g)] + prior,
                      lambda e: e.tensor_tensor(above[:, :, :, :], lj, li, ALU.is_gt))
            dve.step(("rank eq", g), [("logit in", g)] + prior,
                      lambda e: e.tensor_tensor(same[:, :, :, :], lj, li, ALU.is_equal))
            pool.step(("rank before", g), [("rank eq", g), "tri"], lambda e: e.tensor_tensor(
                same[:, :, :, :], same[:, :, :, :], tri[:, :, :].unsqueeze(1).to_broadcast([P, GT, E, E]), ALU.mult))
            pool.step(("rank add", g), [("rank before", g), ("rank gt", g)], lambda e: e.tensor_tensor(
                above[:, :, :, :], above[:, :, :, :], same[:, :, :, :], ALU.add))
            dve.step(("gate max", g), [("logit in", g)], lambda e: e.tensor_reduce(m, l, AX.X, ALU.max))
            dve.step(("gate shift", g), [("gate max", g)], lambda e: e.tensor_tensor(
                x_, l, m.unsqueeze(2).to_broadcast([P, GT, E]), ALU.subtract))
            act.step(("gate exp", g), [("gate shift", g)], lambda e: e.activation(x_, x_, ACT.Exp))

        def gate_weights(g):
            dve.step(("rank", g), [("rank add", g)], lambda e: e.tensor_reduce(
                rank[:, :, :], above[:, :, :, :], AX.X, ALU.add))
            dve.step(("picked", g), [("rank", g), ("gate exp", g)], lambda e: e.scalar_tensor_tensor(
                picked[:, :, :], rank[:, :, :], 1.5, expo[:, g % 2], ALU.is_lt, ALU.mult))
            dve.step(("picked sum", g), [("picked", g)], lambda e: e.tensor_reduce(
                picked_sum[:, :], picked[:, :, :], AX.X, ALU.add))
            dve.step(("picked inverse", g), [("picked sum", g)], lambda e: e.reciprocal(
                picked_inv[:, :], picked_sum[:, :]))
            dve.step(("comb 1", g), [("picked inverse", g)], lambda e: e.tensor_tensor(
                picked[:, :, :], picked[:, :, :], picked_inv[:, :].unsqueeze(2).to_broadcast([P, GT, E]), ALU.mult))
            dve.step(("comb", g), [("comb 1", g)] + ([("y scaled", g - 2, E - 1)] if g >= 2 else []),
                     lambda e: e.tensor_scalar(comb[:, g % 2], picked[:, :, :], out_scale[:, 1:2], None, ALU.mult))

        def hidden_product(g, x_):
            for c in range(HC):
                n = ("hid", g, x_, c)
                cols = slice(c * P, (c + 1) * P)
                pe.step(n, take(n, ("hid H", g, x_, c)) + [("x2T L", g), ("W1 parts", "L")],
                        lambda e, n=n, cols=cols: three_passes(
                            e, bk(n)[:, :], (w1H[:, x_, cols], w1L[:, x_, cols]),
                            (x2tH[:, g % 2, :], x2tL[:, g % 2, :])))

        def hidden_relu(g, x_):
            for c in range(HC):
                n = ("hid", g, x_, c)
                k = (g * E + x_) * HC + c
                free = [("hid L",) + unit(k - NR)] if k >= NR else []
                act.step(("hid relu", g, x_, c), [n, "b1col"] + free, lambda e, n=n, k=k, c=c: e.activation(
                    hid[:, k % NR, :], bk(n)[:, :], ACT.Relu, bias=b1col[:, x_, c:c + 1]))
                m = g * E + x_
                free = [("y",) + ((m - 2) // E, (m - 2) % E)] if m >= 2 else []
                act.step(("hid H", g, x_, c), [n, "b1col"] + free, lambda e, n=n, m=m, c=c: e.activation(
                    hidH[:, m % 2, c, :], bk(n)[:, :], ACT.Relu, bias=b1col[:, x_, c:c + 1]))

        def unit(k):
            return k // (E * HC), k // HC % E, k % HC

        def hidden_low(g, x_):
            for c in range(HC):
                k = (g * E + x_) * HC + c
                m = g * E + x_
                pool.step(("hid L", g, x_, c), [("hid H", g, x_, c)], lambda e, k=k, c=c, m=m: e.tensor_tensor(
                    hidL[:, m % 2, c, :], hid[:, k % NR, :], hidH[:, m % 2, c, :], ALU.subtract))

        def expert_out(g, x_):
            n = ("y", g, x_)
            m = g * E + x_

            def work(e):
                e.matmul(bk(n)[:, :].rearrange("p (t d) -> p t d", t=GT), kilo2[:, :],
                         b2rows[:, x_, :].unsqueeze(1).to_broadcast([2, GT, D]),
                         start=True, stop=False, skip_group_check=True)
                for t in range(GT):
                    for c in range(HC):
                        lhs = [h[:, m % 2, c, t * P:(t + 1) * P] for h in (hidH, hidL)]
                        last = three_passes(e, bk(n)[:, t * D:(t + 1) * D], lhs,
                                            (w2H[:, x_, c, :], w2L[:, x_, c, :]), start=False, stop=(c == HC - 1))
                return last
            pe.step(n, take(n, ("y scaled", g, x_)) + [("hid L", g, x_, 1), ("W2 parts", "L"), "b2rows", "kilo2"], work)

        def expert_scale(g, x_):
            n, m = ("y", g, x_), g * E + x_
            free = [("y add",) + ((m - 2) // E, (m - 2) % E)] if m >= 2 else []
            dve.step(("y scaled", g, x_), [n, ("comb", g)] + free, lambda e: e.tensor_tensor(
                y_scaled[:, m % 2], bk(n)[:, :].rearrange("p (t d) -> p t d", t=GT),
                comb[:, g % 2, :, x_].unsqueeze(2).to_broadcast([P, GT, D]), ALU.mult))

        def expert_add(g, x_):
            m = g * E + x_
            after = [("y add", g, x_ - 1)] if x_ else [("LN", 1, g, "rows")]
            acc = x2[:, g % NX2]
            pool.step(("y add", g, x_), [("y scaled", g, x_)] + after, lambda e: e.tensor_tensor(
                acc, acc, y_scaled[:, m % 2], ALU.add))

        def store(g):
            sp.dma(("store", g), s_load["out"][g % 2], [("y add", g, E - 1)],
                   out[GB * g:GB * (g + 1)].rearrange("(t b) q d -> (b q) t d", b=2), x2[:, g % NX2])

        def within(i, n):
            return 0 <= i < n

        load_x(0)
        load_weights()
        load_ctx(0)
        load_mask(0)
        load_x(1)
        load_ctx(1)
        load_x(2)
        constants()
        for f in norm_steps(0, 0, x_raw[:, 0], xhat[:, :, :], [("x", 0)], []):
            f()
        prepare_weights()
        transpose_group("xT", 0, xhat, [("LN", 0, 0, "rows")], xtH[:, 0, :], xtL[:, 0, :], [])
        FIRST, FFN_LAG = -GB, 2 * GB + 2
        for s in range(FIRST, B + FFN_LAG + GB + 3):
            g, i = s // GB, s % GB
            eg, ei = (s - FFN_LAG) // GB, (s - FFN_LAG) % GB
            hg, hi = (s - 1 - FFN_LAG) // GB, (s - 1 - FFN_LAG) % GB
            pg, pi = (s - 2 - FFN_LAG) // GB, (s - 2 - FFN_LAG) % GB
            for line in (pe, act, dve, pool):
                line.slot = s - FIRST + 1
            if i == 0:
                if within(g + 1, GROUPS) and g + 1 >= 1:
                    load_mask(g + 1)
                if within(g + 2, GROUPS) and g + 2 >= 2:
                    load_ctx(g + 2)
                if within(g + 3, GROUPS) and g + 3 >= 3:
                    load_x(g + 3)
            if within(pg, GROUPS):
                expert_scale(pg, pi)
                expert_add(pg, pi)
                if pi == E - 1:
                    store(pg)
            if within(s - 1, B):
                softmax_sum(s - 1)
                softmax_inverse(s - 1)
                softmax_normal(s - 1)
            if s % 2 == 0 and within((s - 6) // 2, TILES):
                residual((s - 6) // 2)
            if within(s, B):
                scores(s)
                softmax_max(s)
                softmax_shift(s)
                softmax_exp(s)
            if within(g + 1, GROUPS):
                project_queries(g + 1, 2 * i)
                project_queries(g + 1, 2 * i + 1)
            if within(eg, GROUPS):
                hidden_product(eg, ei)
                hidden_relu(eg, ei)
                hidden_low(eg, ei)
            if within(s - 2, B):
                transpose_probs(s - 2)
                probs_high(s - 2)
                probs_low(s - 2)
            if s % 2 == 0 and within(s // 2, TILES):
                project_values(s // 2)
                values_parts(s // 2)
            if within(s - 3, B):
                probs_values(s - 3)
                heads_parts(s - 3)
            if s % 2 == 1 and within((s - 1) // 2, TILES):
                values_place((s - 1) // 2)
            if s % 2 == 1 and within((s - 5) // 2, TILES):
                project_out((s - 5) // 2)
            if within(hg, GROUPS):
                expert_out(hg, hi)
            if within(g + 2, GROUPS) and i in (3, 4, 5):
                if i == 3:
                    pending = norm_steps(0, g + 2, x_raw[:, (g + 2) % NX], xhat[:, :, :],
                                         [("x", g + 2)], [("xT", g + 1)])
                    pending[0]()
                if i == 4:
                    pending[1]()
                    pending[2]()
                if i == 5:
                    pending[3]()
            if within(g + 2, GROUPS) and i == 6:
                transpose_group("xT", g + 2, xhat, [("LN", 0, g + 2, "rows")], xtH[:, g % 2, :],
                                xtL[:, g % 2, :], [("Q", g, H - 1)] if g >= 0 else [])
            if within(g + 1, GROUPS) and i == 5:
                mask_split(g + 1)
            if within(g + 1, GROUPS) and i == 6:
                transpose_group("ctxT", g + 1, ctx_raw[:, (g + 1) % 2], [("ctx", g + 1)],
                                ctH[:, (g + 1) % 2, :], ctL[:, (g + 1) % 2, :],
                                [("scores", GB * g - 1), ("V", GT * g - 1, 1)] if g >= 1 else [])
            if within(g - 1, GROUPS):
                if i == 4:
                    pending2 = norm_steps(1, g - 1, x2[:, (g - 1) % NX2], x2hat[:, :, :],
                                          [("residual", GT * g - 1)], [("x2T", g - 2)] if g >= 2 else [])
                    pending2[0]()
                    pending2[1]()
                if i == 5:
                    pending2[2]()
                    pending2[3]()
                if i == 6:
                    transpose_group("x2T", g - 1, x2hat, [("LN", 1, g - 1, "rows")],
                                    x2tH[:, (g - 1) % 2, :], x2tL[:, (g - 1) % 2, :],
                                    [("hid", g - 3, E - 1, 1)] if g >= 3 else [])
                if i == 7:
                    gate_logits(g - 1)
            if within(g - 2, GROUPS):
                if i == 0:
                    gate_rows(g - 2)
                if i == 1:
                    gate_weights(g - 2)

        for line in (pe, act, dve, pool):
            line.number()

        block = stack.enter_context(nc.Block())

        @block.sync
        def _(eng):
            sp.emit(eng)
            for name in (("store", GROUPS - 2), ("store", GROUPS - 1)):
                eng.wait_ge(*done[name])

        @block.tensor
        def _(eng):
            pe.emit(eng)

        @block.scalar
        def _(eng):
            act.emit(eng)

        @block.vector
        def _(eng):
            dve.emit(eng)

        @block.gpsimd
        def _(eng):
            pool.emit(eng)


_INS = ["x", "ctx_1024", "fside_Bx1xSxS2_0", "g_xattn", "g_ffn", "L0_xattn_Wq", "L0_xattn_Wk",
        "L0_xattn_Wv", "L0_xattn_Wo", "L0_ffn_Wg", "L0_ffn_bg", "L0_ffn_W1", "L0_ffn_b1",
        "L0_ffn_W2", "L0_ffn_b2"]


def kernel(**inputs):
    import numpy as _np
    import concourse.bacc as _bacc
    from concourse import mybir as _mybir
    from concourse.bass_utils import run_bass_kernel_spmd as _run

    nc = _bacc.Bacc("TRN2", target_bir_lowering=False, num_devices=1)
    arrays, args = {}, []
    for name in _INS:
        a = _np.ascontiguousarray(inputs[name])
        arrays[f"in_{name}"] = a
        args.append(nc.dram_tensor(f"in_{name}", a.shape, _mybir.dt.from_np(a.dtype), kind="ExternalInput").ap())
    out = nc.dram_tensor("out_x", (B, S, D), F32, kind="ExternalOutput").ap()
    flamingo_block(nc, *args, out)
    r = _run(nc, [arrays], core_ids=[0])
    return r.results[0]["out_x"]
```

```python
from contextlib import ExitStack

import concourse.bass as bass
from concourse import mybir

F32 = mybir.dt.float32
F32R = mybir.dt.float32r
F16 = mybir.dt.float16
ALU = mybir.AluOpType
ACT = mybir.ActivationFunctionType
AX = mybir.AxisListType

B, S, D = 128, 64, 128
H, DV = 16, 64
E, HID = 8, 256
EPS = 1e-5
P = 128
N = 512
NBANK = 8
TILES = B // 2
GT = N // P
GB = N // S
GROUPS = B // GB
FFN_LAG = 2 * GB
JG = H // 2
C = H * DV // P
HC = HID // P
POOL_HEADS = ((1, 3), (0, 1, 3), (0, 1, 3))
WS = 32.0


PE_ORDER = ("Q 0", "V 1", "V 0", "PT", "Q 1", "scores", "PV", "hid 1", "hid 0", "Wo", "y")
ACT_ORDER = ("V H", "PT out", "PT H", "Q out 1", "Q H 1", "O H", "hid H 1", "hid H 0", "hid relu 0", "Q out 0",
             "hid relu 1", "xT H", "ctxT H", "x2T H", "Q H 0", "exp")
DVE_ORDER = ("y add", "residual", "y scaled", "xT L", "ctxT L", "Q L 0", "sum", "x2T L", "V L", "inverse", "max",
             "hid L 1", "Q L 1", "shift", "V place", "O L")
POOL_ORDER = ("y add", "Q L 0", "Q L 1", "PT L", "normal", "hid L 0", "hid L 1")
PE_LATER = {}
ACT_LATER = {"Q H 0": -1}
DVE_LATER = {"x2T L": 1, "ctxT L": 1, "xT L": 1, "V place": -1, "y add": 1}
POOL_LATER = {"y add": 1, "Q L 0": 1, "Q L 1": 1}


class Line:

    def __init__(self, sem, done, order, later):
        self.sem, self.done, self.steps = sem, done, []
        self.rank = {kind: n for n, kind in enumerate(order)}
        self.later, self.slot, self.queued = later, 0, []

    def step(self, name, after, work):
        slot, rank = self.slot, 0
        if slot:
            halved = f"{name[0]} {name[-1] % 2}" if isinstance(name[-1], int) else ""
            kind = halved if halved in self.rank else name[0]
            slot, rank = slot + self.later.get(kind, 0), self.rank.get(kind, len(self.rank))
        self.queued.append((slot, rank, name, after, work))

    def number(self):
        self.queued.sort(key=lambda q: q[:2])
        for _, _, name, after, work in self.queued:
            self.steps.append((after, work))
            assert name not in self.done, name
            self.done[name] = (self.sem, len(self.steps))

    def emit(self, eng):
        passed = {}
        for after, work in self.steps:
            for name in after:
                sem, count = self.done[name]
                if passed.get(sem.name, 0) < count:
                    passed[sem.name] = count
                    eng.wait_ge(sem, count)
            work(eng).then_inc(self.sem, 1)


class Loads:

    def __init__(self, done):
        self.done, self.steps, self.count = done, [], {}

    def dma(self, name, sem, after, out, in_):
        self.count[sem.name] = self.count.get(sem.name, 0) + 16
        self.done[name] = (sem, self.count[sem.name])
        self.steps.append((after, sem, out, in_))

    def emit(self, eng):
        passed = {}
        for after, sem, out, in_ in self.steps:
            for name in after:
                wait_sem, count = self.done[name]
                if passed.get(wait_sem.name, 0) < count:
                    passed[wait_sem.name] = count
                    eng.wait_ge(wait_sem, count)
            eng.dma_start(out, in_).then_inc(sem, 16)


def flamingo_block(nc, x, ctx, mask, g_xattn, g_ffn, Wq, Wk, Wv, Wo, Wg, bg, W1, b1, W2, b2, out):
    stack = ExitStack()
    with stack:
        def sb(name, shape, dt=F32):
            return stack.enter_context(nc.sbuf_tensor(name, shape, dt))

        def sem(name):
            return stack.enter_context(nc.semaphore(name))

        ident = sb("ident", [P, P])
        spread = sb("spread", [P, P], F32R)
        tri = sb("tri", [P, E, E])
        aH, aL = (sb(f"a{p}", [P, H, D], F16) for p in "HL")
        wvH, wvL = (sb(f"wv{p}", [P, H * DV], F16) for p in "HL")
        woH, woL = (sb(f"wo{p}", [P, C, D], F16) for p in "HL")
        w1H, w1L = (sb(f"w1{p}", [P, E, HID], F16) for p in "HL")
        w2H, w2L = (sb(f"w2{p}", [P, E, HC, D], F16) for p in "HL")
        wgH, wgL = (sb(f"wg{p}", [P, E], F16) for p in "HL")
        b1col = sb("b1col", [P, E, HC])
        b2rows = sb("b2rows", [2, E, D], F32R)
        kilo2 = sb("kilo2", [2, P], F32R)
        bgrow = sb("bgrow", [P, E])
        gates = sb("gates", [P, 2])
        tanh_gates = sb("tanh_gates", [P, 2])
        out_scale = sb("out_scale", [P, 2])

        NX = 4
        x_raw = sb("x_raw", [P, NX, GT, D])
        ctx_raw = sb("ctx_raw", [P, 2, GT, D])
        mask_raw = sb("mask_raw", [P, GB, S])
        mask_parts = sb("mask_parts", [P, 2, GB, S], F32R)
        stats = sb("stats", [P, 2, GT, 6])
        meanvar = sb("meanvar", [P, 2, GT, 2])
        rstd = sb("rstd", [P, 2, GT])
        minus_half = sb("minus_half", [P, GT])
        xhat = sb("xhat", [P, GT, D])
        x2hat = sb("x2hat", [P, GT, D])
        xtH, xtL = (sb(f"xt{p}", [P, 2, N], F16) for p in "HL")
        ctH, ctL = (sb(f"ct{p}", [P, 2, N], F16) for p in "HL")
        x2tH, x2tL = (sb(f"x2t{p}", [P, 2, N], F16) for p in "HL")
        qH, qL = (sb(f"q{p}", [P, 2, JG, GB, 2, S], F16) for p in "HL")
        NX2 = 3
        x2 = sb("x2", [P, NX2, GT, D])

        NPB = 3
        prob = sb("prob", [P, NPB, JG, S])
        row_max = sb("row_max", [P, NPB, JG])
        row_sum = sb("row_sum", [P, NPB, JG])
        row_inv = sb("row_inv", [P, NPB, JG])
        pt = sb("pt", [P, 2, N])
        ptH, ptL = (sb(f"pt{p}", [P, 2, N], F16) for p in "HL")
        vH, vL = (sb(f"v{p}", [P, C, 2, DV], F16) for p in "HL")
        vdH, vdL = (sb(f"vd{p}", [P, 2, 2, C, 2, DV], F16) for p in "HL")
        otH, otL = (sb(f"ot{p}", [P, 2, C, 2, S], F16) for p in "HL")

        logit_t = sb("logit_t", [E, N])
        logit = sb("logit", [P, 2, GT, E])
        logit_max = sb("logit_max", [P, 2, GT])
        expo = sb("expo", [P, 2, GT, E])
        above = sb("above", [P, GT, E, E])
        same = sb("same", [P, GT, E, E])
        rank = sb("rank", [P, GT, E])
        picked = sb("picked", [P, GT, E])
        picked_sum = sb("picked_sum", [P, GT])
        picked_inv = sb("picked_inv", [P, GT])
        comb = sb("comb", [P, 2, GT, E])
        NR = 3
        hid = sb("hid", [P, NR, N])
        hidH, hidL = (sb(f"hid{p}", [P, 2, HC, N], F16) for p in "HL")
        y_scaled = sb("y_scaled", [P, 2, GT, D])

        def as_f32(tensor, pattern):
            return tensor.rearrange(pattern).bitcast(F32)

        q_bytes = [as_f32(q[:, :, :, :, :, :], "p a b c d e -> p (a b c d e)") for q in (qH, qL)]
        wq_raw = q_bytes[0][0:DV, 0:2048].rearrange("p (h d) -> p h d", h=H)
        wk_raw = q_bytes[0][0:DV, 2048:4096].rearrange("p (h d) -> p h d", h=H)
        wv_raw = q_bytes[1][:, 0:1024].rearrange("p (c d) -> p c d", c=C)
        wo_raw = q_bytes[1][:, 1024:2048].rearrange("p (c d) -> p c d", c=C)
        b1_raw = q_bytes[1][0:E * HC, 2048:2048 + P]
        wg_raw = q_bytes[1][:, 2176:2176 + E]
        b2_raw = q_bytes[1][0:2, 4096:5120].rearrange("p (e d) -> p e d", e=E)
        b2_low = q_bytes[1][0:2, 5120:6144].rearrange("p (e d) -> p e d", e=E)
        w1_raw = [as_f32(h[:, :, :, :], "p a c n -> p (a c n)").rearrange("p (e n) -> p e n", e=E // 2)
                  for h in (hidH, hidL)]
        w2_raw = [v.rearrange("p (e c d) -> p e c d", e=E // 2, c=HC) for v in (
            y_scaled[:, :, :, :].rearrange("p a t d -> p (a t d)"),
            x2[:, 1:3, :, :].rearrange("p a t d -> p (a t d)"))]

        bank = [stack.enter_context(nc.psum_tensor(f"bank{i}", [P, N], F32)) for i in range(NBANK)]

        done = {}
        pe = Line(sem("pe_steps"), done, PE_ORDER, PE_LATER)
        act = Line(sem("act_steps"), done, ACT_ORDER, ACT_LATER)
        dve = Line(sem("dve_steps"), done, DVE_ORDER, DVE_LATER)
        pool = Line(sem("pool_steps"), done, POOL_ORDER, POOL_LATER)
        sp = Loads(done)
        s_load = {k: [sem(f"load_{k}{i}") for i in range(n)]
                  for k, n in (("x", NX), ("ctx", 2), ("mask", 1), ("w", 16), ("out", 2))}

        freed_by, bank_of = {}, {}

        def in_bank(name, *last_readers):
            freed_by[name] = last_readers
            return name

        def allot_banks():
            taken = []
            pe.queued.sort(key=lambda q: q[:2])
            for _, _, name, after, _ in pe.queued:
                bank_of[name] = bank[len(taken) % NBANK]
                if len(taken) >= NBANK:
                    after += freed_by[taken[-NBANK]]
                taken.append(name)

        def bk(name):
            return bank_of[name]

        def load_weights():
            half = E // 2
            loads = [
                ("b2", b2_raw, b2.unsqueeze(0).to_broadcast([2, E, D])),
                ("Wq", wq_raw, Wq.rearrange("(h e) d -> e h d", h=H)),
                ("Wk", wk_raw, Wk.rearrange("(h e) d -> e h d", h=H)),
                ("x", None, None),
                ("Wv", wv_raw, Wv.rearrange("(c p) d -> p c d", p=P)),
                ("Wo", wo_raw, Wo.rearrange("d (c p) -> d c p", p=P)),
                ("Wg", wg_raw, Wg),
                ("b1", b1_raw, b1.rearrange("e (c p) -> (e c) p", p=P)),
                ("ctx", None, None),
                ("W1a", w1_raw[0], W1[:half].rearrange("e d n -> d e n")),
                ("W1b", w1_raw[1], W1[half:].rearrange("e d n -> d e n")),
                ("W2a", w2_raw[0], W2[:half].rearrange("e (c p) d -> p e c d", p=P)),
                ("W2b", w2_raw[1], W2[half:].rearrange("e (c p) d -> p e c d", p=P)),
                ("bg", bgrow[:, :], bg.unsqueeze(0).to_broadcast([P, E])),
                ("g_xattn", gates[:, 0:1], g_xattn.unsqueeze(0).to_broadcast([P, 1])),
                ("g_ffn", gates[:, 1:2], g_ffn.unsqueeze(0).to_broadcast([P, 1])),
            ]
            for n, (name, dst, src) in enumerate(loads):
                if name == "x":
                    load_x(0)
                elif name == "ctx":
                    load_x(1)
                    load_ctx(0)
                    load_mask(0)
                else:
                    sp.dma(name, s_load["w"][n], [], dst, src)

        def constants():
            pool.step("ident zero", [], lambda e: e.memset(ident[:, :], 0.0))
            pool.step("ident", ["ident zero"], lambda e: e.affine_select(
                out=ident[:, :], in_=ident[:, :], compare_op=ALU.not_equal, fill=1.0, base=0,
                pattern=[[-1, P]], channel_multiplier=1))
            pool.step("tri one", [], lambda e: e.memset(tri[:, :, :], 1.0))
            pool.step("tri", ["tri one"], lambda e: e.affine_select(
                out=tri[:, :, :], in_=tri[:, :, :], compare_op=ALU.is_gt, fill=0.0, base=0,
                pattern=[[1, E], [-1, E]], channel_multiplier=0))
            pool.step("minus_half", [], lambda e: e.memset(minus_half[:, :], -0.5))
            pool.step("V zero H", [], lambda e: e.memset(vdH[:, :, :, :, :, :], 0.0))
            pool.step("V zero L", [], lambda e: e.memset(vdL[:, :, :, :, :, :], 0.0))

            def spread_work(e):
                for half in (slice(0, S), slice(S, P)):
                    for col in (slice(0, S), slice(S, P)):
                        last = e.tensor_scalar(spread[half, col], ident[half, half], WS, None, ALU.mult)
                return last
            dve.step("spread", ["ident"], spread_work)
            dve.step("kilo2", ["ident"], lambda e: e.tensor_scalar(
                kilo2[:, :], ident[0:2, :], 0.0, WS * WS, ALU.mult, ALU.add))

        def gate_scales():
            act.step("tanh gates", ["g_xattn", "g_ffn"], lambda e: e.activation(
                tanh_gates[:, :], gates[:, :], ACT.Tanh))
            dve.step("out_scale", ["tanh gates"], lambda e: e.tensor_scalar(
                out_scale[:, :], tanh_gates[:, :], 1.0 / (WS * WS), None, ALU.mult))

        def parts_of(name, src, after, dst_high, dst_low, scale=WS):
            act.step((name, "H"), after, lambda e: e.activation(dst_high, src(), ACT.Copy, scale=scale))
            dve.step((name, "L"), [(name, "H")], lambda e: e.scalar_tensor_tensor(
                dst_low, src(), scale, dst_high, ALU.mult, ALU.subtract))

        def prepare_weights():
            for n in range(H // 4):
                name = ("A", n)

                def work(e, n=n, name=name):
                    for i in range(4):
                        last = e.matmul(bk(name)[:, i * D:(i + 1) * D], wq_raw[:, 4 * n + i, :],
                                        wk_raw[:, 4 * n + i, :], start=True, stop=True)
                    return last
                pe.step(in_bank(name, (name, "L")), ["Wq", "Wk"], work)
                flat = [a[:, 4 * n:4 * n + 4, :].rearrange("p h d -> p (h d)") for a in (aH, aL)]
                parts_of(name, lambda name=name: bk(name)[:, :], [name], *flat)
            for what, raw, high, low in (("Wv", wv_raw, wvH[:, :], wvL[:, :]),
                                         ("Wo", wo_raw, woH[:, :, :].rearrange("p c d -> p (c d)"),
                                          woL[:, :, :].rearrange("p c d -> p (c d)"))):
                for n in range(C // 4):
                    name = (what + "T", n)

                    def work(e, n=n, name=name, raw=raw):
                        for i in range(4):
                            last = e.transpose(bk(name)[:, i * P:(i + 1) * P], raw[:, 4 * n + i, :], ident[:, :])
                        return last
                    pe.step(in_bank(name, (name, "L")), [what, "ident"], work)
                    parts_of(name, lambda name=name: bk(name)[:, :], [name],
                             high[:, n * N:(n + 1) * N], low[:, n * N:(n + 1) * N])
            pe.step(in_bank("b1T", "b1col"), ["b1", "ident"], lambda e: e.transpose(
                bk("b1T")[:, 0:E * HC], b1_raw, ident[0:E * HC, 0:E * HC]))
            act.step("b1col", ["b1T"], lambda e: e.activation(
                b1col[:, :, :].rearrange("p e c -> p (e c)"), bk("b1T")[:, 0:E * HC], ACT.Copy, scale=WS))
            parts_of("Wg parts", lambda: wg_raw, ["Wg"], wgH[:, :], wgL[:, :])

        def prepare_b2():
            dve.step("b2 high", ["b2"], lambda e: e.tensor_copy(b2rows[:, :, :], b2_raw))
            dve.step("b2 low", ["b2 high"], lambda e: e.tensor_tensor(
                b2_low, b2_raw, b2rows[:, :, :], ALU.subtract))
            dve.step("b2 row 1", ["b2 low", "ident"], lambda e: e.tensor_scalar(
                b2_low, b2_low, ident[0:2, 1:2], None, ALU.mult))
            dve.step("b2rows", ["b2 row 1"], lambda e: e.scalar_tensor_tensor(
                b2rows[:, :, :], b2rows[:, :, :], ident[0:2, 0:1], b2_low, ALU.mult, ALU.add))

        def prepare_expert_weights(which, half):
            n = (which, "ab"[half])
            some = slice(half * (E // 2), (half + 1) * (E // 2))
            if which == "W1":
                parts_of(n, lambda: w1_raw[half].rearrange("p e n -> p (e n)"), [which + "ab"[half]],
                         *(w[:, some, :].rearrange("p e n -> p (e n)") for w in (w1H, w1L)))
            else:
                parts_of(n, lambda: w2_raw[half].rearrange("p e c d -> p (e c d)"), [which + "ab"[half]],
                         *(w[:, some, :, :].rearrange("p e c d -> p (e c d)") for w in (w2H, w2L)))

        w1_parts, w2_parts = ([((w, x_), "L") for x_ in "ab"] for w in ("W1", "W2"))

        weights_read = [[((w, n), "L") for w, m in (("A", H // 4), ("WvT", C // 4), ("WoT", C // 4))
                         for n in range(m)] + ["b1col", ("Wg parts", "L")],
                        ["b2rows"]]

        def load_x(g):
            after = [("residual", GT * (g - NX) + GT - 1)] if g >= NX else []
            sp.dma(("x", g), s_load["x"][g % NX], after, x_raw[:, g % NX, :, :],
                   x[GB * g:GB * (g + 1)].rearrange("(t b) q d -> (b q) t d", b=2))

        def load_ctx(g):
            after = [("ctxT", g - 2)] if g >= 2 else []
            sp.dma(("ctx", g), s_load["ctx"][g % 2], after, ctx_raw[:, g % 2, :, :],
                   ctx[GB * g:GB * (g + 1)].rearrange("(t b) q d -> (b q) t d", b=2))

        def load_mask(g):
            after = [("mask low", g - 1)] if g >= 1 else []
            for half in range(2):
                sp.dma(("mask", g, half), s_load["mask"][0], after, mask_raw[half * S:(half + 1) * S, :, :],
                       mask[GB * g:GB * (g + 1), 0].rearrange("b q k -> q b k"))

        def mask_split(g):
            parts = mask_parts[:, g % 2, :, :]
            dve.step(("mask high", g), [("mask", g, 0), ("mask", g, 1)]
                     + ([("scores", GB * (g - 1) - 1)] if g >= 2 else []),
                     lambda e: e.tensor_copy(parts, mask_raw[:, :, :]))
            dve.step(("mask low", g), [("mask high", g)], lambda e: e.tensor_tensor(
                parts[S:P], mask_raw[S:P, :, :], parts[S:P], ALU.subtract))

        def norm_steps(which, g, src, dst, after, dst_free):
            st, mv, rs = stats[:, which], meanvar[:, which], rstd[:, which]
            n = ("LN", which, g)

            def stats_work(e):
                for t in range(GT):
                    last = e.bn_stats(st[:, t, :], src[:, t, :])
                return last

            def aggr_work(e):
                for t in range(GT):
                    last = e.bn_aggr(mv[:, t, :], st[:, t, :])
                return last

            def rows_work(e):
                for t in range(GT):
                    last = e.tensor_scalar(dst[:, t, :], src[:, t, :], mv[:, t, 0:1], rs[:, t:t + 1],
                                           ALU.subtract, ALU.mult)
                return last
            prior = [("LN", which, g - 1, "rows")] if g else []
            return [
                lambda: dve.step(n + ("stats",), after + prior, stats_work),
                lambda: dve.step(n + ("aggr",), [n + ("stats",)], aggr_work),
                lambda: (
                    dve.step(n + ("var",), [n + ("aggr",)], lambda e: e.tensor_scalar(
                        rs, mv[:, :, 1], EPS, None, ALU.add)),
                    pool.step(n + ("rstd",), [n + ("var",), "minus_half"], lambda e: e.tensor_tensor(
                        rs, rs, minus_half[:, :], ALU.pow))),
                lambda: dve.step(n + ("rows",), [n + ("rstd",)] + dst_free, rows_work),
            ]

        def transpose_group(name, g, src, after, high, low, free):
            n = (name, g)

            def work(e):
                for t in range(GT):
                    last = e.transpose(bk(n)[:, t * P:(t + 1) * P], src[:, t, :], ident[:, :])
                return last
            pe.step(in_bank(n, (name + " L", g)), after + ["ident"], work)
            act.step((name + " H", g), [n] + free, lambda e: e.activation(high, bk(n)[:, :], ACT.Copy))
            dve.step((name + " L", g), [(name + " H", g)], lambda e: e.tensor_tensor(
                low, bk(n)[:, :], high, ALU.subtract))

        def three_passes(e, dst, lhs, rhs, start=True, stop=True):
            e.matmul(dst, lhs[0], rhs[0], start=start, stop=False, skip_group_check=True)
            e.matmul(dst, lhs[0], rhs[1], start=False, stop=False, skip_group_check=True)
            return e.matmul(dst, lhs[1], rhs[0], start=False, stop=stop, skip_group_check=True)

        def staged(g, h):
            return (g, h) in stages

        stages = [(g, h) for g in range(FFN_LAG // GB + 1) for h in range(H) if h % 4 in POOL_HEADS[g]]

        def project_queries(g, h):
            n = ("Q", g, h)
            j, h2, g2 = h // 4, h % 4 // 2, h % 2
            after = [("xT L", g)] + ([(("A", h // 4), "L")])
            by_pool = staged(g, h)
            last_readers = [("Q H", g, h), ("Q out", g, h) if by_pool else ("Q L", g, h)]
            pe.step(in_bank(n, *last_readers), after, lambda e: three_passes(
                e, bk(n)[:, :], (aH[:, h, :], aL[:, h, :]), (xtH[:, g % 2, :], xtL[:, g % 2, :])))
            dst = [q[:, g % 2, 2 * j + g2, :, h2, :] for q in (qH, qL)]
            src = lambda: bk(n)[:, :].rearrange("p (b q) -> p b q", b=GB)
            free = [("scores", GB * (g - 1) - 1)] if g >= 2 else weights_read[g]
            act.step(("Q H", g, h), [n] + free, lambda e: e.activation(dst[0], src(), ACT.Copy))
            if by_pool:
                k = stages.index((g, h))
                copy = hid[:, k % NR, :].rearrange("p (b q) -> p b q", b=GB)
                act.step(("Q out", g, h), [n] + ([("Q L",) + stages[k - NR]] if k >= NR else []),
                         lambda e: e.activation(copy, src(), ACT.Copy))
                pool.step(("Q L", g, h), [("Q H", g, h), ("Q out", g, h)], lambda e: e.tensor_tensor(
                    dst[1], copy, dst[0], ALU.subtract))
            else:
                dve.step(("Q L", g, h), [("Q H", g, h)], lambda e: e.tensor_tensor(
                    dst[1], src(), dst[0], ALU.subtract))

        def scores(b):
            n = ("scores", b)
            g, i = b // GB, b % GB

            def work(e):
                cols = slice(i * S, (i + 1) * S)
                e.matmul(bk(n)[:, :].rearrange("p (j k) -> p j k", j=JG), spread[:, :],
                         mask_parts[:, g % 2, i, :].unsqueeze(1).to_broadcast([P, JG, S]),
                         start=True, stop=False, skip_group_check=True)
                for jg in range(JG):
                    lhs = [q[:, g % 2, jg, i, :, :].rearrange("p a q -> p (a q)") for q in (qH, qL)]
                    last = three_passes(e, bk(n)[:, jg * S:(jg + 1) * S], lhs,
                                        (ctH[:, g % 2, cols], ctL[:, g % 2, cols]), start=False)
                return last
            pe.step(in_bank(n, ("shift", b)), [("Q L", g, H - 2), ("Q L", g, H - 1), ("ctxT L", g), ("mask low", g), "spread"], work)

        def softmax_max(b):
            src = lambda: bk(("scores", b))[:, :].rearrange("p (j k) -> p j k", j=JG)
            dve.step(("max", b), [("scores", b)] + ([("shift", b - NPB)] if b >= NPB else []),
                     lambda e: e.tensor_reduce(row_max[:, b % NPB, :], src(), AX.X, ALU.max))

        def softmax_shift(b):
            src = lambda: bk(("scores", b))[:, :].rearrange("p (j k) -> p j k", j=JG)
            dve.step(("shift", b), [("max", b)] + ([("PT", b - NPB)] if b >= NPB else []),
                     lambda e: e.tensor_tensor(
                         prob[:, b % NPB, :, :], src(),
                         row_max[:, b % NPB, :].unsqueeze(2).to_broadcast([P, JG, S]), ALU.subtract))

        def softmax_exp(b):
            p = prob[:, b % NPB, :, :]
            act.step(("exp", b), [("shift", b)], lambda e: e.activation(p, p, ACT.Exp, scale=1.0 / WS))

        def softmax_sum(b):
            p = prob[:, b % NPB, :, :]
            dve.step(("sum", b), [("exp", b)] + ([("inverse", b - NPB)] if b >= NPB else []),
                     lambda e: e.tensor_reduce(row_sum[:, b % NPB, :], p, AX.X, ALU.add))

        def softmax_inverse(b):
            dve.step(("inverse", b), [("sum", b)] + ([("normal", b - NPB)] if b >= NPB else []),
                     lambda e: e.reciprocal(row_inv[:, b % NPB, :], row_sum[:, b % NPB, :]))

        def softmax_normal(b):
            p = prob[:, b % NPB, :, :]
            pool.step(("normal", b), [("inverse", b)], lambda e: e.tensor_tensor(
                p, p, row_inv[:, b % NPB, :].unsqueeze(2).to_broadcast([P, JG, S]), ALU.mult))

        def transpose_probs(b):
            n = ("PT", b)

            def work(e):
                p = prob[:, b % NPB, :, :].rearrange("p j k -> p (j k)")
                for j in range(4):
                    last = e.transpose(bk(n)[:, j * P:(j + 1) * P], p[:, j * P:(j + 1) * P], ident[:, :])
                return last
            pe.step(in_bank(n, ("PT H", b), ("PT out", b)), [("normal", b)], work)

        def probs_high(b):
            act.step(("PT H", b), [("PT", b)] + ([("PV", b - 2)] if b >= 2 else []),
                     lambda e: e.activation(ptH[:, b % 2, :], bk(("PT", b))[:, :], ACT.Copy))
            act.step(("PT out", b), [("PT", b)] + ([("PT L", b - 2)] if b >= 2 else []),
                     lambda e: e.activation(pt[:, b % 2, :], bk(("PT", b))[:, :], ACT.Copy))

        def probs_low(b):
            pool.step(("PT L", b), [("PT H", b), ("PT out", b)], lambda e: e.tensor_tensor(
                ptL[:, b % 2, :], pt[:, b % 2, :], ptH[:, b % 2, :], ALU.subtract))

        def project_values(t, half):
            g, i = t // GT, t % GT
            n = ("V", t, half)
            cols = slice(half * N, (half + 1) * N)
            pe.step(in_bank(n, ("V L", t, half)), [("ctxT L", g), (("WvT", 1), "L")],
                    lambda e: three_passes(
                        e, bk(n)[:, :], [c[:, g % 2, i * P:(i + 1) * P] for c in (ctH, ctL)],
                        (wvH[:, cols], wvL[:, cols])))
            dst = [v[:, 4 * half:4 * half + 4, :, :].rearrange("p c g d -> p (c g d)") for v in (vH, vL)]
            act.step(("V H", t, half), [n] + ([("V place", t - 1)] if t else []),
                     lambda e: e.activation(dst[0], bk(n)[:, :], ACT.Copy))
            dve.step(("V L", t, half), [("V H", t, half)], lambda e: e.tensor_tensor(
                dst[1], bk(n)[:, :], dst[0], ALU.subtract))

        def values_place(t):
            def work(e):
                for src, dst in ((vH, vdH), (vL, vdL)):
                    for b2 in range(2):
                        for g2 in range(2):
                            last = e.tensor_copy(dst[g2 * S:(g2 + 1) * S, t % 2, b2, :, g2, :],
                                                 src[b2 * S:(b2 + 1) * S, :, g2, :])
                return last
            dve.step(("V place", t), [("V L", t, 0), ("V L", t, 1), "V zero H", "V zero L"]
                     + ([("PV", 2 * t - 3)] if t >= 2 else []), work)

        def probs_values(b):
            n = ("PV", b)
            t = b // 2

            def work(e):
                for c in range(C):
                    cols = slice(c * S, (c + 1) * S)
                    lhs = [v[:, t % 2, b % 2, c, :, :].rearrange("p g d -> p (g d)") for v in (vdH, vdL)]
                    last = three_passes(e, bk(n)[:, cols], lhs, (ptH[:, b % 2, cols], ptL[:, b % 2, cols]))
                return last
            pe.step(in_bank(n, ("O L", b)), [("PT L", b), ("V place", t)], work)

        def heads_parts(b):
            t = b // 2
            dst = [o[:, t % 2, :, b % 2, :] for o in (otH, otL)]
            src = lambda: bk(("PV", b))[:, :].rearrange("p (c q) -> p c q", c=C)
            act.step(("O H", b), [("PV", b)] + ([("Wo", t - 2)] if t >= 2 else []),
                     lambda e: e.activation(dst[0], src(), ACT.Copy))
            dve.step(("O L", b), [("O H", b)], lambda e: e.tensor_tensor(dst[1], src(), dst[0], ALU.subtract))

        def project_out(t):
            n = ("Wo", t)

            def work(e):
                for c in range(C):
                    lhs = [o[:, t % 2, c, :, :].rearrange("p b q -> p (b q)") for o in (otH, otL)]
                    last = three_passes(e, bk(n)[:, 0:D], lhs, (woH[:, c, :], woL[:, c, :]),
                                        start=(c == 0), stop=(c == C - 1))
                return last
            pe.step(in_bank(n, ("residual", t)), [("O L", 2 * t + 1), (("WoT", 1), "L")], work)

        def residual(t):
            g, i = t // GT, t % GT
            free = [("store", g - NX2)] if g >= NX2 else w2_parts
            dve.step(("residual", t), [("Wo", t), ("x", g), "out_scale"] + free,
                     lambda e: e.scalar_tensor_tensor(x2[:, g % NX2, i, :], bk(("Wo", t))[:, 0:D],
                                                      out_scale[:, 0:1], x_raw[:, g % NX, i, :],
                                                      ALU.mult, ALU.add))

        def gate_logits(g):
            n = ("logitT", g)
            pe.step(in_bank(n, ("logitT out", g)), [("x2T L", g), ("Wg parts", "L")],
                    lambda e: three_passes(e, bk(n)[0:E, :], (wgH[:, :], wgL[:, :]),
                                           (x2tH[:, g % 2, :], x2tL[:, g % 2, :])))
            act.step(("logitT out", g), [n] + ([("logit", g - 1)] if g else []),
                     lambda e: e.activation(logit_t[:, :], bk(n)[0:E, :], ACT.Copy, scale=1.0 / WS))

        def gate_rows(g):
            n = ("logit", g)

            def work(e):
                for t in range(GT):
                    last = e.transpose(bk(n)[:, t * E:(t + 1) * E], logit_t[:, t * P:(t + 1) * P], ident[0:E, 0:E])
                return last
            pe.step(in_bank(n, ("logit in", g)), [("logitT out", g)], work)
            l, m, x_ = logit[:, g % 2], logit_max[:, g % 2], expo[:, g % 2]
            dve.step(("logit in", g), [n, "bg"] + ([("rank eq", g - 2), ("gate shift", g - 2)] if g >= 2 else []),
                     lambda e: e.tensor_tensor(
                         l, bk(n)[:, 0:GT * E].rearrange("p (t e) -> p t e", t=GT),
                         bgrow[:, :].unsqueeze(1).to_broadcast([P, GT, E]), ALU.add))
            prior = [("picked", g - 1)] if g else []
            lj = l.unsqueeze(2).to_broadcast([P, GT, E, E])
            li = l.unsqueeze(3).to_broadcast([P, GT, E, E])
            dve.step(("rank gt", g), [("logit in", g)] + prior,
                      lambda e: e.tensor_tensor(above[:, :, :, :], lj, li, ALU.is_gt))
            dve.step(("rank eq", g), [("logit in", g)] + prior,
                      lambda e: e.tensor_tensor(same[:, :, :, :], lj, li, ALU.is_equal))
            pool.step(("rank before", g), [("rank eq", g), "tri"], lambda e: e.tensor_tensor(
                same[:, :, :, :], same[:, :, :, :], tri[:, :, :].unsqueeze(1).to_broadcast([P, GT, E, E]), ALU.mult))
            pool.step(("rank add", g), [("rank before", g), ("rank gt", g)], lambda e: e.tensor_tensor(
                above[:, :, :, :], above[:, :, :, :], same[:, :, :, :], ALU.add))
            dve.step(("gate max", g), [("logit in", g)], lambda e: e.tensor_reduce(m, l, AX.X, ALU.max))
            dve.step(("gate shift", g), [("gate max", g)], lambda e: e.tensor_tensor(
                x_, l, m.unsqueeze(2).to_broadcast([P, GT, E]), ALU.subtract))
            act.step(("gate exp", g), [("gate shift", g)], lambda e: e.activation(x_, x_, ACT.Exp))

        def gate_weights(g):
            dve.step(("rank", g), [("rank add", g)], lambda e: e.tensor_reduce(
                rank[:, :, :], above[:, :, :, :], AX.X, ALU.add))
            dve.step(("picked", g), [("rank", g), ("gate exp", g)], lambda e: e.scalar_tensor_tensor(
                picked[:, :, :], rank[:, :, :], 1.5, expo[:, g % 2], ALU.is_lt, ALU.mult))
            dve.step(("picked sum", g), [("picked", g)], lambda e: e.tensor_reduce(
                picked_sum[:, :], picked[:, :, :], AX.X, ALU.add))
            dve.step(("picked inverse", g), [("picked sum", g)], lambda e: e.reciprocal(
                picked_inv[:, :], picked_sum[:, :]))
            dve.step(("comb 1", g), [("picked inverse", g)], lambda e: e.tensor_tensor(
                picked[:, :, :], picked[:, :, :], picked_inv[:, :].unsqueeze(2).to_broadcast([P, GT, E]), ALU.mult))
            dve.step(("comb", g), [("comb 1", g)] + ([("y scaled", g - 2, E - 1)] if g >= 2 else []),
                     lambda e: e.tensor_scalar(comb[:, g % 2], picked[:, :, :], out_scale[:, 1:2], None, ALU.mult))

        def hidden_product(g, x_):
            for c in range(HC):
                n = ("hid", g, x_, c)
                cols = slice(c * P, (c + 1) * P)
                pe.step(in_bank(n, ("hid relu", g, x_, c), ("hid H", g, x_, c)), [("x2T L", g), *w1_parts],
                        lambda e, n=n, cols=cols: three_passes(
                            e, bk(n)[:, :], (w1H[:, x_, cols], w1L[:, x_, cols]),
                            (x2tH[:, g % 2, :], x2tL[:, g % 2, :])))

        def hidden_relu(g, x_):
            for c in range(HC):
                n = ("hid", g, x_, c)
                k = (g * E + x_) * HC + c
                free = [("hid L",) + unit(k - NR) if k >= NR else ("Q L",) + stages[k - NR]]
                act.step(("hid relu", g, x_, c), [n, "b1col"] + free, lambda e, n=n, k=k, c=c: e.activation(
                    hid[:, k % NR, :], bk(n)[:, :], ACT.Relu, bias=b1col[:, x_, c:c + 1]))
                m = g * E + x_
                free = [("y",) + ((m - 2) // E, (m - 2) % E)] if m >= 2 else []
                act.step(("hid H", g, x_, c), [n, "b1col", *w1_parts] + free, lambda e, n=n, m=m, c=c: e.activation(
                    hidH[:, m % 2, c, :], bk(n)[:, :], ACT.Relu, bias=b1col[:, x_, c:c + 1]))

        def unit(k):
            return k // (E * HC), k // HC % E, k % HC

        def hidden_low(g, x_, tail):
            for c in range(HC):
                k = (g * E + x_) * HC + c
                m = g * E + x_
                line = dve if tail and c == 1 else pool
                line.step(("hid L", g, x_, c), [("hid relu", g, x_, c), ("hid H", g, x_, c)], lambda e, k=k, c=c, m=m: e.tensor_tensor(
                    hidL[:, m % 2, c, :], hid[:, k % NR, :], hidH[:, m % 2, c, :], ALU.subtract))

        def expert_out(g, x_):
            n = ("y", g, x_)
            m = g * E + x_

            def work(e):
                e.matmul(bk(n)[:, :].rearrange("p (t d) -> p t d", t=GT), kilo2[:, :],
                         b2rows[:, x_, :].unsqueeze(1).to_broadcast([2, GT, D]),
                         start=True, stop=False, skip_group_check=True)
                for t in range(GT):
                    for c in range(HC):
                        lhs = [h[:, m % 2, c, t * P:(t + 1) * P] for h in (hidH, hidL)]
                        last = three_passes(e, bk(n)[:, t * D:(t + 1) * D], lhs,
                                            (w2H[:, x_, c, :], w2L[:, x_, c, :]), start=False, stop=(c == HC - 1))
                return last
            pe.step(in_bank(n, ("y scaled", g, x_)), [("hid L", g, x_, 0), ("hid L", g, x_, 1), "b2rows", "kilo2", *w2_parts], work)

        def expert_scale(g, x_):
            n, m = ("y", g, x_), g * E + x_
            free = [("y add",) + ((m - 2) // E, (m - 2) % E)] if m >= 2 else []
            dve.step(("y scaled", g, x_), [n, ("comb", g), *w2_parts] + free, lambda e: e.tensor_tensor(
                y_scaled[:, m % 2], bk(n)[:, :].rearrange("p (t d) -> p t d", t=GT),
                comb[:, g % 2, :, x_].unsqueeze(2).to_broadcast([P, GT, D]), ALU.mult))

        def expert_add(g, x_, tail):
            m = g * E + x_
            after = [("y add", g, x_ - 1)] if x_ else [("LN", 1, g, "rows")]
            acc = x2[:, g % NX2]
            (dve if tail else pool).step(("y add", g, x_), [("y scaled", g, x_)] + after, lambda e: e.tensor_tensor(
                acc, acc, y_scaled[:, m % 2], ALU.add))

        def store(g):
            sp.dma(("store", g), s_load["out"][g % 2], [("y add", g, E - 1)],
                   out[GB * g:GB * (g + 1)].rearrange("(t b) q d -> (b q) t d", b=2), x2[:, g % NX2])

        def within(i, n):
            return 0 <= i < n

        load_weights()
        load_ctx(1)
        load_x(2)
        constants()
        prepare_b2()
        for f in norm_steps(0, 0, x_raw[:, 0], xhat[:, :, :], [("x", 0)], []):
            f()
        prepare_weights()
        transpose_group("xT", 0, xhat, [("LN", 0, 0, "rows")], xtH[:, 0, :], xtL[:, 0, :], [])
        FIRST = -GB
        for s in range(FIRST, B + FFN_LAG + GB + 3):
            g, i = s // GB, s % GB
            eg, ei = (s - FFN_LAG) // GB, (s - FFN_LAG) % GB
            hg, hi = (s - 1 - FFN_LAG) // GB, (s - 1 - FFN_LAG) % GB
            pg, pi = (s - 2 - FFN_LAG) // GB, (s - 2 - FFN_LAG) % GB
            for line in (pe, act, dve, pool):
                line.slot = s - FIRST + 1
            if i == 0:
                if within(g + 1, GROUPS) and g + 1 >= 1:
                    load_mask(g + 1)
                if within(g + 2, GROUPS) and g + 2 >= 2:
                    load_ctx(g + 2)
                if within(g + 3, GROUPS) and g + 3 >= 3:
                    load_x(g + 3)
            if within(pg, GROUPS):
                expert_scale(pg, pi)
                expert_add(pg, pi, s >= B + 4)
                if pi == E - 1:
                    store(pg)
            if s == 1:
                gate_scales()
            if s in (2, 3, 4, 5):
                prepare_expert_weights(("W1", "W2")[s // 4], s % 2)
            if within(s - 1, B):
                softmax_sum(s - 1)
                softmax_inverse(s - 1)
                softmax_normal(s - 1)
            if s % 2 == 0 and within((s - 6) // 2, TILES):
                residual((s - 6) // 2)
            if within(s, B):
                scores(s)
                softmax_max(s)
                softmax_shift(s)
                softmax_exp(s)
            if within(g + 1, GROUPS):
                project_queries(g + 1, 2 * i)
                project_queries(g + 1, 2 * i + 1)
            if within(s // 2, TILES):
                project_values(s // 2, s % 2)
            if within(eg, GROUPS):
                hidden_product(eg, ei)
                hidden_relu(eg, ei)
                hidden_low(eg, ei, s >= B + 2)
            if within(s - 2, B):
                transpose_probs(s - 2)
                probs_high(s - 2)
                probs_low(s - 2)
            if within(s - 3, B):
                probs_values(s - 3)
                heads_parts(s - 3)
            if s % 2 == 0 and within((s - 2) // 2, TILES):
                values_place((s - 2) // 2)
            if s % 2 == 1 and within((s - 5) // 2, TILES):
                project_out((s - 5) // 2)
            if within(hg, GROUPS):
                expert_out(hg, hi)
            sooner = 2 if s < 0 else 0
            if within(g + 2, GROUPS):
                if i == 3 - sooner:
                    pending = norm_steps(0, g + 2, x_raw[:, (g + 2) % NX], xhat[:, :, :],
                                         [("x", g + 2)], [("xT", g + 1)])
                    pending[0]()
                if i == 4 - sooner:
                    pending[1]()
                    pending[2]()
                if i == 5 - sooner:
                    pending[3]()
            if within(g + 2, GROUPS) and i == 6:
                transpose_group("xT", g + 2, xhat, [("LN", 0, g + 2, "rows")], xtH[:, g % 2, :],
                                xtL[:, g % 2, :], [("Q", g, H - 2), ("Q", g, H - 1)] if g >= 0 else [])
            if within(g + 1, GROUPS) and i == 5 - sooner:
                mask_split(g + 1)
            if within(g + 1, GROUPS) and i == 6 - sooner:
                transpose_group("ctxT", g + 1, ctx_raw[:, (g + 1) % 2], [("ctx", g + 1)],
                                ctH[:, (g + 1) % 2, :], ctL[:, (g + 1) % 2, :],
                                [("scores", GB * g - 1), ("V", GT * g - 1, 0), ("V", GT * g - 1, 1)] if g >= 1 else [])
            if within(g - 1, GROUPS):
                if i == 4:
                    pending2 = norm_steps(1, g - 1, x2[:, (g - 1) % NX2], x2hat[:, :, :],
                                          [("residual", GT * g - 1)], [("x2T", g - 2)] if g >= 2 else [])
                    pending2[0]()
                    pending2[1]()
                if i == 5:
                    pending2[2]()
                    pending2[3]()
                if i == 6:
                    transpose_group("x2T", g - 1, x2hat, [("LN", 1, g - 1, "rows")],
                                    x2tH[:, (g - 1) % 2, :], x2tL[:, (g - 1) % 2, :],
                                    [("hid", g - 3, E - 1, 0), ("hid", g - 3, E - 1, 1)] if g >= 3 else [])
                if i == 7:
                    gate_logits(g - 1)
            if within(g - 2, GROUPS):
                if i == 0:
                    gate_rows(g - 2)
                if i == 1:
                    gate_weights(g - 2)

        allot_banks()
        for line in (pe, act, dve, pool):
            line.number()

        block = stack.enter_context(nc.Block())

        @block.sync
        def _(eng):
            sp.emit(eng)
            for name in (("store", GROUPS - 2), ("store", GROUPS - 1)):
                eng.wait_ge(*done[name])

        @block.tensor
        def _(eng):
            pe.emit(eng)

        @block.scalar
        def _(eng):
            act.emit(eng)

        @block.vector
        def _(eng):
            dve.emit(eng)

        @block.gpsimd
        def _(eng):
            pool.emit(eng)


_INS = ["x", "ctx_1024", "fside_Bx1xSxS2_0", "g_xattn", "g_ffn", "L0_xattn_Wq", "L0_xattn_Wk",
        "L0_xattn_Wv", "L0_xattn_Wo", "L0_ffn_Wg", "L0_ffn_bg", "L0_ffn_W1", "L0_ffn_b1",
        "L0_ffn_W2", "L0_ffn_b2"]


def kernel(**inputs):
    import numpy as _np
    import concourse.bacc as _bacc
    from concourse import mybir as _mybir
    from concourse.bass_utils import run_bass_kernel_spmd as _run

    nc = _bacc.Bacc("TRN2", target_bir_lowering=False, num_devices=1)
    arrays, args = {}, []
    for name in _INS:
        a = _np.ascontiguousarray(inputs[name])
        arrays[f"in_{name}"] = a
        args.append(nc.dram_tensor(f"in_{name}", a.shape, _mybir.dt.from_np(a.dtype), kind="ExternalInput").ap())
    out = nc.dram_tensor("out_x", (B, S, D), F32, kind="ExternalOutput").ap()
    flamingo_block(nc, *args, out)
    r = _run(nc, [arrays], core_ids=[0])
    return r.results[0]["out_x"]
```

```python
from contextlib import ExitStack

import concourse.bass as bass
from concourse import mybir

F32 = mybir.dt.float32
F32R = mybir.dt.float32r
F16 = mybir.dt.float16
ALU = mybir.AluOpType
ACT = mybir.ActivationFunctionType
AX = mybir.AxisListType

B, S, D = 128, 64, 128
H, DV = 16, 64
E, HID = 8, 256
EPS = 1e-5
P = 128
N = 512
NBANK = 8
TILES = B // 2
GT = N // P
GB = N // S
GROUPS = B // GB
FFN_LAG = 2 * GB
JG = H // 2
C = H * DV // P
BIAS_AT = 1
CL = 4
HC = HID // P
POOL_HEADS = ((1, 3), (0, 1, 3), (0, 1, 3))
WS = 32.0


PE_ORDER = ("Q 0", "V 0", "V 1", "Q 1", "scores", "PT", "hid 0", "PV", "hid 1", "Wo", "y")
ACT_ORDER = ("Q H 0", "V H", "exp", "Q H 1", "Q out 1", "PT H", "PT out", "hid relu 0", "O H", "Q out 0",
             "hid H 0", "hid relu 1", "hid H 1", "x2T H", "xT H", "ctxT H")
DVE_ORDER = ("y scaled", "x2T L", "residual", "xT L", "ctxT L", "b2 add", "Q L 0", "V L", "y add", "sum",
             "Q L 1", "max", "inverse", "hid L 1", "shift", "O L")
POOL_ORDER = ("Q L 1", "hid L 1", "y add", "PT L", "normal", "Q L 0", "hid L 0")
PE_LATER = {}
ACT_LATER = {"exp": 1}
DVE_LATER = {"x2T L": 1, "ctxT L": 1, "xT L": 1, "y add": 1}
POOL_LATER = {"y add": 1, "hid L 1": 1}


class Line:

    def __init__(self, sem, done, order, later):
        self.sem, self.done, self.steps = sem, done, []
        self.rank = {kind: n for n, kind in enumerate(order)}
        self.later, self.slot, self.queued = later, 0, []

    def step(self, name, after, work):
        slot, rank = self.slot, 0
        if slot:
            halved = f"{name[0]} {name[-1] % 2}" if isinstance(name[-1], int) else ""
            kind = halved if halved in self.rank else name[0]
            slot, rank = slot + self.later.get(kind, 0), self.rank.get(kind, len(self.rank))
        self.queued.append((slot, rank, name, after, work))

    def number(self):
        self.queued.sort(key=lambda q: q[:2])
        for _, _, name, after, work in self.queued:
            self.steps.append((after, work))
            assert name not in self.done, name
            self.done[name] = (self.sem, len(self.steps))

    def emit(self, eng):
        passed = {}
        for after, work in self.steps:
            for name in after:
                sem, count = self.done[name]
                if passed.get(sem.name, 0) < count:
                    passed[sem.name] = count
                    eng.wait_ge(sem, count)
            work(eng).then_inc(self.sem, 1)


class Loads:

    def __init__(self, done):
        self.done, self.steps, self.count = done, [], {}

    def dma(self, name, sem, after, out, in_):
        self.count[sem.name] = self.count.get(sem.name, 0) + 16
        self.done[name] = (sem, self.count[sem.name])
        self.steps.append((after, sem, out, in_))

    def emit(self, eng):
        passed = {}
        for after, sem, out, in_ in self.steps:
            for name in after:
                wait_sem, count = self.done[name]
                if passed.get(wait_sem.name, 0) < count:
                    passed[wait_sem.name] = count
                    eng.wait_ge(wait_sem, count)
            eng.dma_start(out, in_).then_inc(sem, 16)


def flamingo_block(nc, x, ctx, mask, g_xattn, g_ffn, Wq, Wk, Wv, Wo, Wg, bg, W1, b1, W2, b2, out):
    stack = ExitStack()
    with stack:
        def sb(name, shape, dt=F32):
            return stack.enter_context(nc.sbuf_tensor(name, shape, dt))

        def sem(name):
            return stack.enter_context(nc.semaphore(name))

        ident = sb("ident", [P, P])
        spread = sb("spread", [P, P], F32R)
        tri = sb("tri", [P, E, E])
        aH, aL = (sb(f"a{p}", [P, H, D], F16) for p in "HL")
        wvH, wvL = (sb(f"wv{p}", [P, 2, C // CL, DV, CL], F16) for p in "HL")
        woH, woL = (sb(f"wo{p}", [P, C, D], F16) for p in "HL")
        w1H, w1L = (sb(f"w1{p}", [P, E, HID], F16) for p in "HL")
        w2H, w2L = (sb(f"w2{p}", [P, E, HC, D], F16) for p in "HL")
        wgH, wgL = (sb(f"wg{p}", [P, E], F16) for p in "HL")
        b1col = sb("b1col", [P, E, HC])
        b2H, b2L = (sb(f"b2{p}", [E, D], F16) for p in "HL")
        bgrow = sb("bgrow", [P, E])
        gates = sb("gates", [P, 2])
        tanh_gates = sb("tanh_gates", [P, 2])
        out_scale = sb("out_scale", [P, 2])

        NX = 4
        x_raw = sb("x_raw", [P, NX, GT, D])
        ctx_raw = sb("ctx_raw", [P, 2, GT, D])
        mask_raw = sb("mask_raw", [P, GB, S])
        mask_parts = sb("mask_parts", [P, 2, GB, S], F32R)
        stats = sb("stats", [P, 2, GT, 6])
        meanvar = sb("meanvar", [P, 2, GT, 2])
        rstd = sb("rstd", [P, 2, GT])
        minus_half = sb("minus_half", [P, GT])
        xhat = sb("xhat", [P, GT, D])
        x2hat = sb("x2hat", [P, GT, D])
        xtH, xtL = (sb(f"xt{p}", [P, 2, N], F16) for p in "HL")
        ctH, ctL = (sb(f"ct{p}", [P, 2, N], F16) for p in "HL")
        x2tH, x2tL = (sb(f"x2t{p}", [P, 2, N], F16) for p in "HL")
        qH, qL = (sb(f"q{p}", [P, 2, JG, GB, 2, S], F16) for p in "HL")
        NX2 = 3
        x2 = sb("x2", [P, NX2, GT, D])

        NPB = 3
        prob = sb("prob", [P, NPB, JG, S])
        row_max = sb("row_max", [P, NPB, JG])
        row_sum = sb("row_sum", [P, NPB, JG])
        row_inv = sb("row_inv", [P, NPB, JG])
        pt = sb("pt", [P, 2, N])
        ptH, ptL = (sb(f"pt{p}", [P, 2, N], F16) for p in "HL")
        vH, vL = (sb(f"v{p}", [P, 2, C // CL, DV, CL], F16) for p in "HL")
        vdH, vdL = (sb(f"vd{p}", [P, 2, 2, C // CL, 2, DV, CL], F16) for p in "HL")
        otH, otL = (sb(f"ot{p}", [P, 2, C, 2, S], F16) for p in "HL")

        logit_t = sb("logit_t", [E, N])
        logit = sb("logit", [P, 2, GT, E])
        logit_max = sb("logit_max", [P, 2, GT])
        expo = sb("expo", [P, 2, GT, E])
        above = sb("above", [P, GT, E, E])
        same = sb("same", [P, GT, E, E])
        rank = sb("rank", [P, GT, E])
        picked = sb("picked", [P, GT, E])
        picked_sum = sb("picked_sum", [P, GT])
        picked_inv = sb("picked_inv", [P, GT])
        comb = sb("comb", [P, 2, GT, E])
        pickedT_H, pickedT_L = (sb(f"pickedT_{p}", [E, N], F16) for p in "HL")
        NR = 3
        hid = sb("hid", [P, NR, N])
        hidH, hidL = (sb(f"hid{p}", [P, 2, HC, N], F16) for p in "HL")
        y_scaled = sb("y_scaled", [P, 2, GT, D])

        def as_f32(tensor, pattern):
            return tensor.rearrange(pattern).bitcast(F32)

        q_bytes = [as_f32(q[:, :, :, :, :, :], "p a b c d e -> p (a b c d e)") for q in (qH, qL)]
        wq_raw = q_bytes[0][0:DV, 0:2048].rearrange("p (h d) -> p h d", h=H)
        wk_raw = q_bytes[0][0:DV, 2048:4096].rearrange("p (h d) -> p h d", h=H)
        wv_raw = q_bytes[1][:, 0:1024].rearrange("p (c d) -> p c d", c=C)
        wo_raw = q_bytes[1][:, 1024:2048].rearrange("p (c d) -> p c d", c=C)
        b1_raw = q_bytes[1][0:E * HC, 2048:2048 + P]
        wg_raw = q_bytes[1][:, 2176:2176 + E]
        b2_raw = q_bytes[1][0:E, 2304:2304 + D]
        w1_raw = [as_f32(h[:, :, :, :], "p a c n -> p (a c n)").rearrange("p (e n) -> p e n", e=E // 2)
                  for h in (hidH, hidL)]
        w2_raw = [v.rearrange("p (e c d) -> p e c d", e=E // 2, c=HC) for v in (
            y_scaled[:, :, :, :].rearrange("p a t d -> p (a t d)"),
            x2[:, 1:3, :, :].rearrange("p a t d -> p (a t d)"))]

        bank = [stack.enter_context(nc.psum_tensor(f"bank{i}", [P, N], F32)) for i in range(NBANK)]

        done = {}
        pe = Line(sem("pe_steps"), done, PE_ORDER, PE_LATER)
        act = Line(sem("act_steps"), done, ACT_ORDER, ACT_LATER)
        dve = Line(sem("dve_steps"), done, DVE_ORDER, DVE_LATER)
        pool = Line(sem("pool_steps"), done, POOL_ORDER, POOL_LATER)
        sp = Loads(done)
        s_place = [[sem(f"place_{buf}_{g2}") for g2 in range(2)] for buf in range(2)]
        s_load = {k: [sem(f"load_{k}{i}") for i in range(n)]
                  for k, n in (("x", NX), ("ctx", 2), ("mask", 1), ("w", 16), ("out", 2))}

        freed_by, bank_of = {}, {}

        def in_bank(name, *last_readers):
            freed_by[name] = last_readers
            return name

        def allot_banks():
            taken = []
            pe.queued.sort(key=lambda q: q[:2])
            for _, _, name, after, _ in pe.queued:
                bank_of[name] = bank[len(taken) % NBANK]
                if len(taken) >= NBANK:
                    after += freed_by[taken[-NBANK]]
                taken.append(name)

        def bk(name):
            return bank_of[name]

        def load_weights():
            half = E // 2
            loads = [
                ("Wq", wq_raw, Wq.rearrange("(h e) d -> e h d", h=H)),
                ("Wk", wk_raw, Wk.rearrange("(h e) d -> e h d", h=H)),
                ("x", None, None),
                ("Wv", wv_raw, Wv.rearrange("(c p) d -> p c d", p=P)),
                ("Wo", wo_raw, Wo.rearrange("d (c p) -> d c p", p=P)),
                ("Wg", wg_raw, Wg),
                ("b2", b2_raw, b2),
                ("b1", b1_raw, b1.rearrange("e (c p) -> (e c) p", p=P)),
                ("ctx", None, None),
                ("W1a", w1_raw[0], W1[:half].rearrange("e d n -> d e n")),
                ("W1b", w1_raw[1], W1[half:].rearrange("e d n -> d e n")),
                ("W2a", w2_raw[0], W2[:half].rearrange("e (c p) d -> p e c d", p=P)),
                ("W2b", w2_raw[1], W2[half:].rearrange("e (c p) d -> p e c d", p=P)),
                ("bg", bgrow[:, :], bg.unsqueeze(0).to_broadcast([P, E])),
                ("g_xattn", gates[:, 0:1], g_xattn.unsqueeze(0).to_broadcast([P, 1])),
                ("g_ffn", gates[:, 1:2], g_ffn.unsqueeze(0).to_broadcast([P, 1])),
            ]
            for n, (name, dst, src) in enumerate(loads):
                if name == "x":
                    load_x(0)
                elif name == "ctx":
                    load_x(1)
                    load_ctx(0)
                    load_mask(0)
                else:
                    sp.dma(name, s_load["w"][n], [], dst, src)

        def constants():
            pool.step("ident zero", [], lambda e: e.memset(ident[:, :], 0.0))
            pool.step("ident", ["ident zero"], lambda e: e.affine_select(
                out=ident[:, :], in_=ident[:, :], compare_op=ALU.not_equal, fill=1.0, base=0,
                pattern=[[-1, P]], channel_multiplier=1))
            pool.step("tri one", [], lambda e: e.memset(tri[:, :, :], 1.0))
            pool.step("tri", ["tri one"], lambda e: e.affine_select(
                out=tri[:, :, :], in_=tri[:, :, :], compare_op=ALU.is_gt, fill=0.0, base=0,
                pattern=[[1, E], [-1, E]], channel_multiplier=0))
            pool.step("minus_half", [], lambda e: e.memset(minus_half[:, :], -0.5))
            pool.step("V zero H", [], lambda e: e.memset(vdH[:, :, :, :, :, :, :], 0.0))
            pool.step("V zero L", [], lambda e: e.memset(vdL[:, :, :, :, :, :, :], 0.0))

            def spread_work(e):
                for half in (slice(0, S), slice(S, P)):
                    for col in (slice(0, S), slice(S, P)):
                        last = e.tensor_scalar(spread[half, col], ident[half, half], WS, None, ALU.mult)
                return last
            dve.step("spread", ["ident"], spread_work)

        def gate_scales():
            act.step("tanh gates", ["g_xattn", "g_ffn"], lambda e: e.activation(
                tanh_gates[:, :], gates[:, :], ACT.Tanh))
            dve.step("out_scale", ["tanh gates"], lambda e: e.tensor_scalar(
                out_scale[:, :], tanh_gates[:, :], 1.0 / (WS * WS), None, ALU.mult))

        def parts_of(name, src, after, dst_high, dst_low, scale=WS):
            act.step((name, "H"), after, lambda e: e.activation(dst_high, src(), ACT.Copy, scale=scale))
            dve.step((name, "L"), [(name, "H")], lambda e: e.scalar_tensor_tensor(
                dst_low, src(), scale, dst_high, ALU.mult, ALU.subtract))

        def prepare_weights():
            for n in range(H // 4):
                name = ("A", n)

                def work(e, n=n, name=name):
                    for i in range(4):
                        last = e.matmul(bk(name)[:, i * D:(i + 1) * D], wq_raw[:, 4 * n + i, :],
                                        wk_raw[:, 4 * n + i, :], start=True, stop=True)
                    return last
                pe.step(in_bank(name, (name, "L")), ["Wq", "Wk"], work)
                flat = [a[:, 4 * n:4 * n + 4, :].rearrange("p h d -> p (h d)") for a in (aH, aL)]
                parts_of(name, lambda name=name: bk(name)[:, :], [name], *flat)
            for what, raw in (("Wv", wv_raw), ("Wo", wo_raw)):
                for n in range(C // CL):
                    name = (what + "T", n)

                    def work(e, n=n, name=name, raw=raw):
                        for i in range(4):
                            last = e.transpose(bk(name)[:, i * P:(i + 1) * P], raw[:, 4 * n + i, :], ident[:, :])
                        return last
                    pe.step(in_bank(name, (name, "L")), [what, "ident"], work)
                    four = slice(4 * n, 4 * n + 4)
                    if what == "Wv":
                        parts_of(name, lambda name=name: bk(name)[:, :].rearrange("p (c g d) -> p g d c", c=CL, g=2),
                                 [name], wvH[:, :, n, :, :], wvL[:, :, n, :, :])
                    else:
                        parts_of(name, lambda name=name: bk(name)[:, :].rearrange("p (c d) -> p c d", c=4),
                                 [name], woH[:, four, :], woL[:, four, :])
            pe.step(in_bank("b1T", "b1col"), ["b1", "ident"], lambda e: e.transpose(
                bk("b1T")[:, 0:E * HC], b1_raw, ident[0:E * HC, 0:E * HC]))
            act.step("b1col", ["b1T"], lambda e: e.activation(
                b1col[:, :, :].rearrange("p e c -> p (e c)"), bk("b1T")[:, 0:E * HC], ACT.Copy, scale=WS))
            parts_of("Wg parts", lambda: wg_raw, ["Wg"], wgH[:, :], wgL[:, :])
            parts_of("b2 parts", lambda: b2_raw, ["b2"], b2H[:, :], b2L[:, :])

        def prepare_expert_weights(which, half):
            n = (which, "ab"[half])
            some = slice(half * (E // 2), (half + 1) * (E // 2))
            if which == "W1":
                parts_of(n, lambda: w1_raw[half].rearrange("p e n -> p (e n)"), [which + "ab"[half]],
                         *(w[:, some, :].rearrange("p e n -> p (e n)") for w in (w1H, w1L)))
            else:
                parts_of(n, lambda: w2_raw[half].rearrange("p e c d -> p (e c d)"), [which + "ab"[half]],
                         *(w[:, some, :, :].rearrange("p e c d -> p (e c d)") for w in (w2H, w2L)))

        w1_parts, w2_parts = ([((w, x_), "L") for x_ in "ab"] for w in ("W1", "W2"))

        weights_read = [[((w, n), "L") for w, m in (("A", H // 4), ("WvT", C // 4), ("WoT", C // 4))
                         for n in range(m)] + ["b1col", ("Wg parts", "L"), ("b2 parts", "L")],
                        []]

        def load_x(g):
            after = [("residual", GT * (g - NX) + GT - 1)] if g >= NX else []
            sp.dma(("x", g), s_load["x"][g % NX], after, x_raw[:, g % NX, :, :],
                   x[GB * g:GB * (g + 1)].rearrange("(t b) q d -> (b q) t d", b=2))

        def load_ctx(g):
            after = [("ctxT", g - 2)] if g >= 2 else []
            sp.dma(("ctx", g), s_load["ctx"][g % 2], after, ctx_raw[:, g % 2, :, :],
                   ctx[GB * g:GB * (g + 1)].rearrange("(t b) q d -> (b q) t d", b=2))

        def load_mask(g):
            after = [("mask low", g - 1)] if g >= 1 else []
            for half in range(2):
                sp.dma(("mask", g, half), s_load["mask"][0], after, mask_raw[half * S:(half + 1) * S, :, :],
                       mask[GB * g:GB * (g + 1), 0].rearrange("b q k -> q b k"))

        def mask_split(g):
            parts = mask_parts[:, g % 2, :, :]
            dve.step(("mask high", g), [("mask", g, 0), ("mask", g, 1)]
                     + ([("scores", GB * (g - 1) - 1)] if g >= 2 else []),
                     lambda e: e.tensor_copy(parts, mask_raw[:, :, :]))
            dve.step(("mask low", g), [("mask high", g)], lambda e: e.tensor_tensor(
                parts[S:P], mask_raw[S:P, :, :], parts[S:P], ALU.subtract))

        def norm_steps(which, g, src, dst, after, dst_free):
            st, mv, rs = stats[:, which], meanvar[:, which], rstd[:, which]
            n = ("LN", which, g)

            def stats_work(e):
                for t in range(GT):
                    last = e.bn_stats(st[:, t, :], src[:, t, :])
                return last

            def aggr_work(e):
                for t in range(GT):
                    last = e.bn_aggr(mv[:, t, :], st[:, t, :])
                return last

            def rows_work(e):
                for t in range(GT):
                    last = e.tensor_scalar(dst[:, t, :], src[:, t, :], mv[:, t, 0:1], rs[:, t:t + 1],
                                           ALU.subtract, ALU.mult)
                return last
            prior = [("LN", which, g - 1, "rows")] if g else []
            return [
                lambda: dve.step(n + ("stats",), after + prior, stats_work),
                lambda: dve.step(n + ("aggr",), [n + ("stats",)], aggr_work),
                lambda: (
                    dve.step(n + ("var",), [n + ("aggr",)], lambda e: e.tensor_scalar(
                        rs, mv[:, :, 1], EPS, None, ALU.add)),
                    pool.step(n + ("rstd",), [n + ("var",), "minus_half"], lambda e: e.tensor_tensor(
                        rs, rs, minus_half[:, :], ALU.pow))),
                lambda: dve.step(n + ("rows",), [n + ("rstd",)] + dst_free, rows_work),
            ]

        def transpose_group(name, g, src, after, high, low, free):
            n = (name, g)

            def work(e):
                for t in range(GT):
                    last = e.transpose(bk(n)[:, t * P:(t + 1) * P], src[:, t, :], ident[:, :])
                return last
            pe.step(in_bank(n, (name + " L", g)), after + ["ident"], work)
            act.step((name + " H", g), [n] + free, lambda e: e.activation(high, bk(n)[:, :], ACT.Copy))
            dve.step((name + " L", g), [(name + " H", g)], lambda e: e.tensor_tensor(
                low, bk(n)[:, :], high, ALU.subtract))

        def three_passes(e, dst, lhs, rhs, start=True, stop=True):
            e.matmul(dst, lhs[0], rhs[0], start=start, stop=False, skip_group_check=True)
            e.matmul(dst, lhs[0], rhs[1], start=False, stop=False, skip_group_check=True)
            return e.matmul(dst, lhs[1], rhs[0], start=False, stop=stop, skip_group_check=True)

        def staged(g, h):
            return (g, h) in stages

        stages = [(g, h) for g in range(FFN_LAG // GB + 1) for h in range(H) if h % 4 in POOL_HEADS[g]]

        def project_queries(g, h):
            n = ("Q", g, h)
            j, h2, g2 = h // 4, h % 4 // 2, h % 2
            after = [("xT L", g)] + ([(("A", h // 4), "L")])
            by_pool = staged(g, h)
            last_readers = [("Q H", g, h), ("Q out", g, h) if by_pool else ("Q L", g, h)]
            pe.step(in_bank(n, *last_readers), after, lambda e: three_passes(
                e, bk(n)[:, :], (aH[:, h, :], aL[:, h, :]), (xtH[:, g % 2, :], xtL[:, g % 2, :])))
            dst = [q[:, g % 2, 2 * j + g2, :, h2, :] for q in (qH, qL)]
            src = lambda: bk(n)[:, :].rearrange("p (b q) -> p b q", b=GB)
            free = [("scores", GB * (g - 1) - 1)] if g >= 2 else weights_read[g]
            act.step(("Q H", g, h), [n] + free, lambda e: e.activation(dst[0], src(), ACT.Copy))
            if by_pool:
                k = stages.index((g, h))
                copy = hid[:, k % NR, :].rearrange("p (b q) -> p b q", b=GB)
                act.step(("Q out", g, h), [n] + ([("Q L",) + stages[k - NR]] if k >= NR else []),
                         lambda e: e.activation(copy, src(), ACT.Copy))
                pool.step(("Q L", g, h), [("Q H", g, h), ("Q out", g, h)], lambda e: e.tensor_tensor(
                    dst[1], copy, dst[0], ALU.subtract))
            else:
                dve.step(("Q L", g, h), [("Q H", g, h)], lambda e: e.tensor_tensor(
                    dst[1], src(), dst[0], ALU.subtract))

        def scores(b):
            n = ("scores", b)
            g, i = b // GB, b % GB

            def work(e):
                cols = slice(i * S, (i + 1) * S)
                e.matmul(bk(n)[:, :].rearrange("p (j k) -> p j k", j=JG), spread[:, :],
                         mask_parts[:, g % 2, i, :].unsqueeze(1).to_broadcast([P, JG, S]),
                         start=True, stop=False, skip_group_check=True)
                for jg in range(JG):
                    lhs = [q[:, g % 2, jg, i, :, :].rearrange("p a q -> p (a q)") for q in (qH, qL)]
                    last = three_passes(e, bk(n)[:, jg * S:(jg + 1) * S], lhs,
                                        (ctH[:, g % 2, cols], ctL[:, g % 2, cols]), start=False)
                return last
            pe.step(in_bank(n, ("shift", b)), [("Q L", g, H - 2), ("Q L", g, H - 1), ("ctxT L", g), ("mask low", g), "spread"], work)

        def softmax_max(b):
            src = lambda: bk(("scores", b))[:, :].rearrange("p (j k) -> p j k", j=JG)
            dve.step(("max", b), [("scores", b)] + ([("shift", b - NPB)] if b >= NPB else []),
                     lambda e: e.tensor_reduce(row_max[:, b % NPB, :], src(), AX.X, ALU.max))

        def softmax_shift(b):
            src = lambda: bk(("scores", b))[:, :].rearrange("p (j k) -> p j k", j=JG)
            dve.step(("shift", b), [("max", b)] + ([("PT", b - NPB)] if b >= NPB else []),
                     lambda e: e.tensor_tensor(
                         prob[:, b % NPB, :, :], src(),
                         row_max[:, b % NPB, :].unsqueeze(2).to_broadcast([P, JG, S]), ALU.subtract))

        def softmax_exp(b):
            p = prob[:, b % NPB, :, :]
            act.step(("exp", b), [("shift", b)], lambda e: e.activation(p, p, ACT.Exp, scale=1.0 / WS))

        def softmax_sum(b):
            p = prob[:, b % NPB, :, :]
            dve.step(("sum", b), [("exp", b)] + ([("inverse", b - NPB)] if b >= NPB else []),
                     lambda e: e.tensor_reduce(row_sum[:, b % NPB, :], p, AX.X, ALU.add))

        def softmax_inverse(b):
            dve.step(("inverse", b), [("sum", b)] + ([("normal", b - NPB)] if b >= NPB else []),
                     lambda e: e.reciprocal(row_inv[:, b % NPB, :], row_sum[:, b % NPB, :]))

        def softmax_normal(b):
            p = prob[:, b % NPB, :, :]
            pool.step(("normal", b), [("inverse", b)], lambda e: e.tensor_tensor(
                p, p, row_inv[:, b % NPB, :].unsqueeze(2).to_broadcast([P, JG, S]), ALU.mult))

        def transpose_probs(b):
            n = ("PT", b)

            def work(e):
                p = prob[:, b % NPB, :, :].rearrange("p j k -> p (j k)")
                for j in range(4):
                    last = e.transpose(bk(n)[:, j * P:(j + 1) * P], p[:, j * P:(j + 1) * P], ident[:, :])
                return last
            pe.step(in_bank(n, ("PT H", b), ("PT out", b)), [("normal", b)], work)

        def probs_high(b):
            act.step(("PT H", b), [("PT", b)] + ([("PV", b - 2)] if b >= 2 else []),
                     lambda e: e.activation(ptH[:, b % 2, :], bk(("PT", b))[:, :], ACT.Copy))
            act.step(("PT out", b), [("PT", b)] + ([("PT L", b - 2)] if b >= 2 else []),
                     lambda e: e.activation(pt[:, b % 2, :], bk(("PT", b))[:, :], ACT.Copy))

        def probs_low(b):
            pool.step(("PT L", b), [("PT H", b), ("PT out", b)], lambda e: e.tensor_tensor(
                ptL[:, b % 2, :], pt[:, b % 2, :], ptH[:, b % 2, :], ALU.subtract))

        def project_values(t, g2):
            g, i = t // GT, t % GT
            n = ("V", t, g2)
            pe.step(in_bank(n, ("V L", t, g2)), [("ctxT L", g), (("WvT", 1), "L")],
                    lambda e: three_passes(
                        e, bk(n)[:, :], [c[:, g % 2, i * P:(i + 1) * P] for c in (ctH, ctL)],
                        [w[:, g2, :, :, :].rearrange("p a d c -> p (a d c)") for w in (wvH, wvL)]))
            dst = [v[:, g2, :, :, :].rearrange("p a d c -> p (a d c)") for v in (vH, vL)]
            act.step(("V H", t, g2), [n] + ([(t - 1, g2)] if t else []),
                     lambda e: e.activation(dst[0], bk(n)[:, :], ACT.Copy))
            dve.step(("V L", t, g2), [("V H", t, g2)], lambda e: e.tensor_tensor(
                dst[1], bk(n)[:, :], dst[0], ALU.subtract))

        def values_place(t, g2):
            after = [("V L", t, g2), "V zero H", "V zero L"] + ([("PV", 2 * t - 4), ("PV", 2 * t - 3)] if t >= 2 else [])
            for part, src, dst in (("H", vH, vdH), ("L", vL, vdL)):
                for b2 in range(2):
                    last = part == "L" and b2 == 1
                    sp.dma((t, g2) if last else (t, g2, part, b2), s_place[t % 2][g2], after,
                           dst[g2 * S:(g2 + 1) * S, t % 2, b2, :, g2].rearrange("p a d c -> p a (d c)"),
                           src[b2 * S:(b2 + 1) * S, g2].rearrange("p a d c -> p a (d c)"))

        def probs_values(b):
            n = ("PV", b)
            t = b // 2

            def work(e):
                for c in range(C):
                    cols = slice(c * S, (c + 1) * S)
                    lhs = [v[:, t % 2, b % 2, c // CL, :, :, c % CL].rearrange("p g d -> p (g d)") for v in (vdH, vdL)]
                    last = three_passes(e, bk(n)[:, cols], lhs, (ptH[:, b % 2, cols], ptL[:, b % 2, cols]))
                return last
            pe.step(in_bank(n, ("O L", b)), [("PT L", b), (t, 0), (t, 1)], work)

        def heads_parts(b):
            t = b // 2
            dst = [o[:, t % 2, :, b % 2, :] for o in (otH, otL)]
            src = lambda: bk(("PV", b))[:, :].rearrange("p (c q) -> p c q", c=C)
            act.step(("O H", b), [("PV", b)] + ([("Wo", t - 2)] if t >= 2 else []),
                     lambda e: e.activation(dst[0], src(), ACT.Copy))
            dve.step(("O L", b), [("O H", b)], lambda e: e.tensor_tensor(dst[1], src(), dst[0], ALU.subtract))

        def project_out(t):
            n = ("Wo", t)

            def work(e):
                for c in range(C):
                    lhs = [o[:, t % 2, c, :, :].rearrange("p b q -> p (b q)") for o in (otH, otL)]
                    last = three_passes(e, bk(n)[:, 0:D], lhs, (woH[:, c, :], woL[:, c, :]),
                                        start=(c == 0), stop=(c == C - 1))
                return last
            pe.step(in_bank(n, ("residual", t)), [("O L", 2 * t + 1), (("WoT", 1), "L")], work)

        def residual(t):
            g, i = t // GT, t % GT
            free = [("store", g - NX2)] if g >= NX2 else w2_parts
            dve.step(("residual", t), [("Wo", t), ("x", g), "out_scale"] + free,
                     lambda e: e.scalar_tensor_tensor(x2[:, g % NX2, i, :], bk(("Wo", t))[:, 0:D],
                                                      out_scale[:, 0:1], x_raw[:, g % NX, i, :],
                                                      ALU.mult, ALU.add))

        def gate_logits(g):
            n = ("logitT", g)
            pe.step(in_bank(n, ("logitT out", g)), [("x2T L", g), ("Wg parts", "L")],
                    lambda e: three_passes(e, bk(n)[0:E, :], (wgH[:, :], wgL[:, :]),
                                           (x2tH[:, g % 2, :], x2tL[:, g % 2, :])))
            act.step(("logitT out", g), [n] + ([("logit", g - 1)] if g else []),
                     lambda e: e.activation(logit_t[:, :], bk(n)[0:E, :], ACT.Copy, scale=1.0 / WS))

        def gate_rows(g):
            n = ("logit", g)

            def work(e):
                for t in range(GT):
                    last = e.transpose(bk(n)[:, t * E:(t + 1) * E], logit_t[:, t * P:(t + 1) * P], ident[0:E, 0:E])
                return last
            pe.step(in_bank(n, ("logit in", g)), [("logitT out", g)], work)
            l, m, x_ = logit[:, g % 2], logit_max[:, g % 2], expo[:, g % 2]
            dve.step(("logit in", g), [n, "bg"] + ([("rank eq", g - 2), ("gate shift", g - 2)] if g >= 2 else []),
                     lambda e: e.tensor_tensor(
                         l, bk(n)[:, 0:GT * E].rearrange("p (t e) -> p t e", t=GT),
                         bgrow[:, :].unsqueeze(1).to_broadcast([P, GT, E]), ALU.add))
            prior = [("picked", g - 1)] if g else []
            lj = l.unsqueeze(2).to_broadcast([P, GT, E, E])
            li = l.unsqueeze(3).to_broadcast([P, GT, E, E])
            dve.step(("rank gt", g), [("logit in", g)] + prior,
                      lambda e: e.tensor_tensor(above[:, :, :, :], lj, li, ALU.is_gt))
            dve.step(("rank eq", g), [("logit in", g)] + prior,
                      lambda e: e.tensor_tensor(same[:, :, :, :], lj, li, ALU.is_equal))
            pool.step(("rank before", g), [("rank eq", g), "tri"], lambda e: e.tensor_tensor(
                same[:, :, :, :], same[:, :, :, :], tri[:, :, :].unsqueeze(1).to_broadcast([P, GT, E, E]), ALU.mult))
            pool.step(("rank add", g), [("rank before", g), ("rank gt", g)], lambda e: e.tensor_tensor(
                above[:, :, :, :], above[:, :, :, :], same[:, :, :, :], ALU.add))
            dve.step(("gate max", g), [("logit in", g)], lambda e: e.tensor_reduce(m, l, AX.X, ALU.max))
            dve.step(("gate shift", g), [("gate max", g)], lambda e: e.tensor_tensor(
                x_, l, m.unsqueeze(2).to_broadcast([P, GT, E]), ALU.subtract))
            act.step(("gate exp", g), [("gate shift", g)], lambda e: e.activation(x_, x_, ACT.Exp))

        def gate_weights(g):
            dve.step(("rank", g), [("rank add", g)], lambda e: e.tensor_reduce(
                rank[:, :, :], above[:, :, :, :], AX.X, ALU.add))
            dve.step(("picked", g), [("rank", g), ("gate exp", g)] + ([("pickedT", g - 1)] if g else []), lambda e: e.scalar_tensor_tensor(
                picked[:, :, :], rank[:, :, :], 1.5, expo[:, g % 2], ALU.is_lt, ALU.mult))
            dve.step(("picked sum", g), [("picked", g)], lambda e: e.tensor_reduce(
                picked_sum[:, :], picked[:, :, :], AX.X, ALU.add))
            dve.step(("picked inverse", g), [("picked sum", g)], lambda e: e.reciprocal(
                picked_inv[:, :], picked_sum[:, :]))
            dve.step(("comb 1", g), [("picked inverse", g)], lambda e: e.tensor_tensor(
                picked[:, :, :], picked[:, :, :], picked_inv[:, :].unsqueeze(2).to_broadcast([P, GT, E]), ALU.mult))
            dve.step(("comb", g), [("comb 1", g)] + ([("y scaled", g - 2, E - 1)] if g >= 2 else []),
                     lambda e: e.tensor_scalar(comb[:, g % 2], picked[:, :, :], out_scale[:, 1:2], None, ALU.mult))

        def bias_out(g):
            n = ("pickedT", g)

            def transposes(e):
                for t in range(GT):
                    last = e.transpose(bk(n)[0:E, t * P:(t + 1) * P], picked[:, t, :], ident[:, :])
                return last
            pe.step(in_bank(n, ("pickedT L", g)), [("comb 1", g)], transposes)
            act.step(("pickedT H", g), [n] + ([("b2 out", g - 1)] if g else []), lambda e: e.activation(
                pickedT_H[:, :], bk(n)[0:E, :], ACT.Copy, scale=WS))
            dve.step(("pickedT L", g), [("pickedT H", g)], lambda e: e.scalar_tensor_tensor(
                pickedT_L[:, :], bk(n)[0:E, :], WS, pickedT_H[:, :], ALU.mult, ALU.subtract))

        def bias_product(g):
            n = ("b2 out", g)

            def work(e):
                for t in range(GT):
                    cols = slice(t * P, (t + 1) * P)
                    last = three_passes(e, bk(n)[:, t * D:(t + 1) * D], (pickedT_H[:, cols], pickedT_L[:, cols]),
                                        (b2H[:, :], b2L[:, :]))
                return last
            pe.step(in_bank(n, ("b2 add", g)), [("pickedT L", g)], work)

        def bias_add(g):
            acc = x2[:, g % NX2]
            dve.step(("b2 add", g), [("b2 out", g), ("y add", g, BIAS_AT - 1)], lambda e: e.scalar_tensor_tensor(
                acc, bk(("b2 out", g))[:, :].rearrange("p (t d) -> p t d", t=GT), out_scale[:, 1:2], acc,
                ALU.mult, ALU.add))

        def hidden_product(g, x_):
            for c in range(HC):
                n = ("hid", g, x_, c)
                cols = slice(c * P, (c + 1) * P)
                pe.step(in_bank(n, ("hid relu", g, x_, c), ("hid H", g, x_, c)), [("x2T L", g), *w1_parts],
                        lambda e, n=n, cols=cols: three_passes(
                            e, bk(n)[:, :], (w1H[:, x_, cols], w1L[:, x_, cols]),
                            (x2tH[:, g % 2, :], x2tL[:, g % 2, :])))

        def hidden_relu(g, x_):
            for c in range(HC):
                n = ("hid", g, x_, c)
                k = (g * E + x_) * HC + c
                free = [("hid L",) + unit(k - NR) if k >= NR else ("Q L",) + stages[k - NR]]
                act.step(("hid relu", g, x_, c), [n, "b1col"] + free, lambda e, n=n, k=k, c=c: e.activation(
                    hid[:, k % NR, :], bk(n)[:, :], ACT.Relu, bias=b1col[:, x_, c:c + 1]))
                m = g * E + x_
                free = [("y",) + ((m - 2) // E, (m - 2) % E)] if m >= 2 else []
                act.step(("hid H", g, x_, c), [n, "b1col", *w1_parts] + free, lambda e, n=n, m=m, c=c: e.activation(
                    hidH[:, m % 2, c, :], bk(n)[:, :], ACT.Relu, bias=b1col[:, x_, c:c + 1]))

        def unit(k):
            return k // (E * HC), k // HC % E, k % HC

        def hidden_low(g, x_, tail):
            for c in range(HC):
                k = (g * E + x_) * HC + c
                m = g * E + x_
                line = dve if tail and c == 1 else pool
                line.step(("hid L", g, x_, c), [("hid relu", g, x_, c), ("hid H", g, x_, c)], lambda e, k=k, c=c, m=m: e.tensor_tensor(
                    hidL[:, m % 2, c, :], hid[:, k % NR, :], hidH[:, m % 2, c, :], ALU.subtract))

        def expert_out(g, x_):
            n = ("y", g, x_)
            m = g * E + x_

            def work(e):
                for t in range(GT):
                    for c in range(HC):
                        lhs = [h[:, m % 2, c, t * P:(t + 1) * P] for h in (hidH, hidL)]
                        last = three_passes(e, bk(n)[:, t * D:(t + 1) * D], lhs,
                                            (w2H[:, x_, c, :], w2L[:, x_, c, :]), start=(c == 0), stop=(c == HC - 1))
                return last
            pe.step(in_bank(n, ("y scaled", g, x_)), [("hid L", g, x_, 0), ("hid L", g, x_, 1), *w2_parts], work)

        def expert_scale(g, x_):
            n, m = ("y", g, x_), g * E + x_
            free = [("y add",) + ((m - 2) // E, (m - 2) % E)] if m >= 2 else []
            dve.step(("y scaled", g, x_), [n, ("comb", g), *w2_parts] + free, lambda e: e.tensor_tensor(
                y_scaled[:, m % 2], bk(n)[:, :].rearrange("p (t d) -> p t d", t=GT),
                comb[:, g % 2, :, x_].unsqueeze(2).to_broadcast([P, GT, D]), ALU.mult))

        def expert_add(g, x_, tail):
            m = g * E + x_
            after = [("y add", g, x_ - 1) if x_ else ("LN", 1, g, "rows")] + ([("b2 add", g)] if x_ == BIAS_AT else [])
            acc = x2[:, g % NX2]
            (dve if tail else pool).step(("y add", g, x_), [("y scaled", g, x_)] + after, lambda e: e.tensor_tensor(
                acc, acc, y_scaled[:, m % 2], ALU.add))

        def store(g):
            sp.dma(("store", g), s_load["out"][g % 2], [("y add", g, E - 1)],
                   out[GB * g:GB * (g + 1)].rearrange("(t b) q d -> (b q) t d", b=2), x2[:, g % NX2])

        def within(i, n):
            return 0 <= i < n

        load_weights()
        load_ctx(1)
        load_x(2)
        constants()
        for f in norm_steps(0, 0, x_raw[:, 0], xhat[:, :, :], [("x", 0)], []):
            f()
        prepare_weights()
        transpose_group("xT", 0, xhat, [("LN", 0, 0, "rows")], xtH[:, 0, :], xtL[:, 0, :], [])
        FIRST = -GB
        for s in range(FIRST, B + FFN_LAG + GB + 3):
            g, i = s // GB, s % GB
            eg, ei = (s - FFN_LAG) // GB, (s - FFN_LAG) % GB
            hg, hi = (s - 1 - FFN_LAG) // GB, (s - 1 - FFN_LAG) % GB
            pg, pi = (s - 2 - FFN_LAG) // GB, (s - 2 - FFN_LAG) % GB
            for line in (pe, act, dve, pool):
                line.slot = s - FIRST + 1
            if i == 0:
                if within(g + 1, GROUPS) and g + 1 >= 1:
                    load_mask(g + 1)
                if within(g + 2, GROUPS) and g + 2 >= 2:
                    load_ctx(g + 2)
            if i == 6 and within(g + 3, GROUPS) and g + 3 >= 3:
                load_x(g + 3)
            if within(pg, GROUPS):
                expert_scale(pg, pi)
                expert_add(pg, pi, s >= B + 4)
            if pi == 1 and within(pg - 1, GROUPS):
                store(pg - 1)
            if s == 1:
                gate_scales()
            if s in (2, 3, 4, 5):
                prepare_expert_weights(("W1", "W2")[s // 4], s % 2)
            if within(s - 1, B):
                softmax_sum(s - 1)
                softmax_inverse(s - 1)
                softmax_normal(s - 1)
            if s % 2 == 0 and within((s - 6) // 2, TILES):
                residual((s - 6) // 2)
            if within(s, B):
                scores(s)
                softmax_max(s)
                softmax_shift(s)
                softmax_exp(s)
            if within(g + 1, GROUPS):
                project_queries(g + 1, 2 * i)
                project_queries(g + 1, 2 * i + 1)
            if within(s // 2, TILES):
                project_values(s // 2, s % 2)
                values_place(s // 2, s % 2)
            if within(eg, GROUPS):
                hidden_product(eg, ei)
                hidden_relu(eg, ei)
                hidden_low(eg, ei, s >= B + 2)
            if within(s - 2, B):
                transpose_probs(s - 2)
                probs_high(s - 2)
                probs_low(s - 2)
            if within(s - 3, B):
                probs_values(s - 3)
                heads_parts(s - 3)
            if s % 2 == 1 and within((s - 5) // 2, TILES):
                project_out((s - 5) // 2)
            if within(hg, GROUPS):
                expert_out(hg, hi)
            sooner = 2 if s < 0 else 0
            if within(g + 2, GROUPS):
                if i == 3 - sooner:
                    pending = norm_steps(0, g + 2, x_raw[:, (g + 2) % NX], xhat[:, :, :],
                                         [("x", g + 2)], [("xT", g + 1)])
                    pending[0]()
                if i == 4 - sooner:
                    pending[1]()
                    pending[2]()
                if i == 5 - sooner:
                    pending[3]()
            if within(g + 2, GROUPS) and i == 6:
                transpose_group("xT", g + 2, xhat, [("LN", 0, g + 2, "rows")], xtH[:, g % 2, :],
                                xtL[:, g % 2, :], [("Q", g, H - 2), ("Q", g, H - 1)] if g >= 0 else [])
            if within(g + 1, GROUPS) and i == 5 - sooner:
                mask_split(g + 1)
            if within(g + 1, GROUPS) and i == 6 - sooner:
                transpose_group("ctxT", g + 1, ctx_raw[:, (g + 1) % 2], [("ctx", g + 1)],
                                ctH[:, (g + 1) % 2, :], ctL[:, (g + 1) % 2, :],
                                [("scores", GB * g - 1), ("V", GT * g - 1, 0), ("V", GT * g - 1, 1)] if g >= 1 else [])
            if within(g - 1, GROUPS):
                if i == 4:
                    pending2 = norm_steps(1, g - 1, x2[:, (g - 1) % NX2], x2hat[:, :, :],
                                          [("residual", GT * g - 1)], [("x2T", g - 2)] if g >= 2 else [])
                    pending2[0]()
                    pending2[1]()
                if i == 5:
                    pending2[2]()
                    pending2[3]()
                if i == 6:
                    transpose_group("x2T", g - 1, x2hat, [("LN", 1, g - 1, "rows")],
                                    x2tH[:, (g - 1) % 2, :], x2tL[:, (g - 1) % 2, :],
                                    [("hid", g - 3, E - 1, 0), ("hid", g - 3, E - 1, 1)] if g >= 3 else [])
                if i == 7:
                    gate_logits(g - 1)
            if within(g - 2, GROUPS):
                if i == 0:
                    gate_rows(g - 2)
                if i == 1:
                    gate_weights(g - 2)
                if i == 2:
                    bias_out(g - 2)
                if i == 3:
                    bias_product(g - 2)
                if i == 4:
                    bias_add(g - 2)

        allot_banks()
        for line in (pe, act, dve, pool):
            line.number()

        block = stack.enter_context(nc.Block())

        @block.sync
        def _(eng):
            sp.emit(eng)
            for name in (("store", GROUPS - 2), ("store", GROUPS - 1)):
                eng.wait_ge(*done[name])

        @block.tensor
        def _(eng):
            pe.emit(eng)

        @block.scalar
        def _(eng):
            act.emit(eng)

        @block.vector
        def _(eng):
            dve.emit(eng)

        @block.gpsimd
        def _(eng):
            pool.emit(eng)


_INS = ["x", "ctx_1024", "fside_Bx1xSxS2_0", "g_xattn", "g_ffn", "L0_xattn_Wq", "L0_xattn_Wk",
        "L0_xattn_Wv", "L0_xattn_Wo", "L0_ffn_Wg", "L0_ffn_bg", "L0_ffn_W1", "L0_ffn_b1",
        "L0_ffn_W2", "L0_ffn_b2"]


def kernel(**inputs):
    import numpy as _np
    import concourse.bacc as _bacc
    from concourse import mybir as _mybir
    from concourse.bass_utils import run_bass_kernel_spmd as _run

    nc = _bacc.Bacc("TRN2", target_bir_lowering=False, num_devices=1)
    arrays, args = {}, []
    for name in _INS:
        a = _np.ascontiguousarray(inputs[name])
        arrays[f"in_{name}"] = a
        args.append(nc.dram_tensor(f"in_{name}", a.shape, _mybir.dt.from_np(a.dtype), kind="ExternalInput").ap())
    out = nc.dram_tensor("out_x", (B, S, D), F32, kind="ExternalOutput").ap()
    flamingo_block(nc, *args, out)
    r = _run(nc, [arrays], core_ids=[0])
    return r.results[0]["out_x"]
```
